# Optimizing a Trainium2 kernel written in Bass

```python
import numpy as np
import jax
import jax.numpy as jnp

def _softmax(x, axis=-1):
    return jax.nn.softmax(x, axis=axis)

def _gelu(x):
    return jax.nn.gelu(x, approximate=True)

def _silu(x):
    return jax.nn.silu(x)

def _sigmoid(x):
    return jax.nn.sigmoid(x)

def _layernorm(x, axis=-1, eps=1e-05):
    m = jnp.mean(x, axis=axis, keepdims=True)
    v = jnp.var(x, axis=axis, keepdims=True)
    return (x - m) / jnp.sqrt(v + eps)

def _scatter_add(tgt, idx, src, axis=0):
    return tgt.at[idx].add(src)

def _segment_sum(src, seg, n):
    return jax.ops.segment_sum(src, seg, n)
kernel_name = 'mk_gnn_preln_d2_gnn_r32_8e1ee1'

def setup_inputs(seed: int=0):
    np.random.seed(seed)
    _w = jnp.asarray

    def _rec_inputs():
        import jax
        import jax.numpy as jnp
        _gk = jax.random.key(seed)
        x = -0.0002928 + 1 * jax.random.normal(jax.random.fold_in(_gk, 1), (256, 512), jnp.float32)
        src = jax.random.randint(jax.random.fold_in(_gk, 2), (4096,), 0, 256, jnp.int32)
        dst = jnp.minimum((256 * jax.random.uniform(jax.random.fold_in(_gk, 3), (4096,)) ** 2.0).astype(jnp.int32), 8191)
        _o = jnp.argsort(dst, stable=True)
        src = src[_o]
        dst = dst[_o]
        edge_attr_20 = 0.000389844 + 1.00025 * jax.random.normal(jax.random.fold_in(_gk, 12), (4096, 20), jnp.float32)
        edge_attr_4 = -0.00185629 + 0.998788 * jax.random.normal(jax.random.fold_in(_gk, 13), (4096, 4), jnp.float32)
        edge_weight = jax.random.uniform(jax.random.fold_in(_gk, 15), (4096,), jnp.float32, 0.0, 0.999993)
        return (x, src, dst, edge_attr_20, edge_attr_4, edge_weight)
    x, src, dst, edge_attr_20, edge_attr_4, edge_weight = _rec_inputs()

    def _L0_gnn_setup():
        import jax, jax.numpy as jnp
        import numpy as np
        N_NODES = 256
        N_EDGES = 8192
        D_IN = 512
        D_OUT = 512
        key = jax.random.key(seed)
        k1, k2, k3 = jax.random.split(key, 3)
        x = jax.random.normal(k1, (N_NODES, D_IN), dtype=jnp.float32)
        edge_index = jax.random.randint(k2, (2, N_EDGES), 0, N_NODES, dtype=jnp.int64)
        weight = jax.random.normal(k3, (D_IN, D_OUT), dtype=jnp.float32)
        bias = jnp.zeros((D_OUT,), dtype=jnp.float32)
        return {'x': x, 'edge_index': edge_index, 'weight': weight, 'bias': bias}
    _L0_gnn_all = _L0_gnn_setup()
    _L0_gnn_in = {k: v for k, v in _L0_gnn_all.items() if k in ('weight', 'bias')}
    del _L0_gnn_all

    def _L1_gnn_setup():
        import jax, jax.numpy as jnp
        import numpy as np
        import math
        B = 128
        F = 32
        R = 20
        N = 512
        E = 8192
        LOG2 = 0.6931471805599453
        IS2 = 1.0 / math.sqrt(2.0)
        IS3 = 1.0 / math.sqrt(3.0)
        IS6 = 1.0 / math.sqrt(6.0)

        def ssp(x):
            return jax.nn.softplus(x) - LOG2
        key = jax.random.key(seed)
        ks = jax.random.split(key, 14)
        return dict(x=jax.random.normal(ks[0], (N, 4 * B), jnp.float32), idx_i=jax.random.randint(ks[1], (E,), 0, N), idx_j=jax.random.randint(ks[2], (E,), 0, N), f_ij=jax.random.normal(ks[3], (E, R), jnp.float32), rcut_ij=jax.random.uniform(ks[4], (E,), jnp.float32), Yr_ij=jax.random.normal(ks[5], (E, 4), jnp.float32), w_in2f_s=jax.random.normal(ks[6], (B, F), jnp.float32), w_in2f_v=jax.random.normal(ks[7], (B, F), jnp.float32), W1=jax.random.normal(ks[8], (R, F), jnp.float32) / math.sqrt(R), b1=jnp.zeros((F,), jnp.float32), W2=jax.random.normal(ks[9], (F, 6 * F), jnp.float32) / math.sqrt(F), b2=jnp.zeros((6 * F,), jnp.float32), w_f2o1_s=jax.random.normal(ks[10], (2 * F, B), jnp.float32), w_f2o1_v=jax.random.normal(ks[11], (2 * F, B), jnp.float32), w_f2o2_s=jax.random.normal(ks[12], (B, B), jnp.float32), w_f2o2_v=jax.random.normal(ks[13], (B, B), jnp.float32))
    _L1_gnn_all = _L1_gnn_setup()
    _L1_gnn_in = {k: v for k, v in _L1_gnn_all.items() if k in ('w_in2f_s', 'w_in2f_v', 'W1', 'b1', 'W2', 'b2', 'w_f2o1_s', 'w_f2o1_v', 'w_f2o2_s', 'w_f2o2_v')}
    del _L1_gnn_all
    return {'x': x, 'src': src, 'dst': dst, 'edge_attr_20': edge_attr_20, 'edge_attr_4': edge_attr_4, 'edge_weight': edge_weight, 'L0_gnn_weight': _L0_gnn_in['weight'], 'L0_gnn_bias': _L0_gnn_in['bias'], 'L1_gnn_w_in2f_s': _L1_gnn_in['w_in2f_s'], 'L1_gnn_w_in2f_v': _L1_gnn_in['w_in2f_v'], 'L1_gnn_W1': _L1_gnn_in['W1'], 'L1_gnn_b1': _L1_gnn_in['b1'], 'L1_gnn_W2': _L1_gnn_in['W2'], 'L1_gnn_b2': _L1_gnn_in['b2'], 'L1_gnn_w_f2o1_s': _L1_gnn_in['w_f2o1_s'], 'L1_gnn_w_f2o1_v': _L1_gnn_in['w_f2o1_v'], 'L1_gnn_w_f2o2_s': _L1_gnn_in['w_f2o2_s'], 'L1_gnn_w_f2o2_v': _L1_gnn_in['w_f2o2_v']}

def reference(x, src, dst, edge_attr_20, edge_attr_4, edge_weight, L0_gnn_weight, L0_gnn_bias, L1_gnn_w_in2f_s, L1_gnn_w_in2f_v, L1_gnn_W1, L1_gnn_b1, L1_gnn_W2, L1_gnn_b2, L1_gnn_w_f2o1_s, L1_gnn_w_f2o1_v, L1_gnn_w_f2o2_s, L1_gnn_w_f2o2_v):
    import jax
    import jax.numpy as jnp

    def _L0_gnn_ref(x, edge_index, weight, bias):
        import jax, jax.numpy as jnp
        import numpy as np
        N_NODES = 256
        N_EDGES = 8192
        D_IN = 512
        D_OUT = 512
        n = x.shape[0]
        adj = jnp.zeros((n, n), dtype=x.dtype)
        adj = adj.at[edge_index[0], edge_index[1]].set(1.0)
        adj = adj.at[edge_index[1], edge_index[0]].set(1.0)
        adj = adj + jnp.eye(n, dtype=x.dtype)
        deg = jnp.sum(adj, axis=1)
        dinv = 1.0 / jnp.sqrt(deg)
        adj = adj * dinv[:, None] * dinv[None, :]
        return adj @ (x @ weight) + bias

    def _L1_gnn_ref(x, idx_i, idx_j, f_ij, rcut_ij, Yr_ij, w_in2f_s, w_in2f_v, W1, b1, W2, b2, w_f2o1_s, w_f2o1_v, w_f2o2_s, w_f2o2_v):
        import jax, jax.numpy as jnp
        import numpy as np
        import math
        B = 128
        F = 32
        R = 20
        N = 512
        E = 8192
        LOG2 = 0.6931471805599453
        IS2 = 1.0 / math.sqrt(2.0)
        IS3 = 1.0 / math.sqrt(3.0)
        IS6 = 1.0 / math.sqrt(6.0)

        def ssp(x):
            return jax.nn.softplus(x) - LOG2
        n = x.shape[0]
        xs = x[:, :B]
        xv = x[:, B:].reshape(n, B, 3)
        hs = xs @ w_in2f_s / math.sqrt(B)
        hv = jnp.einsum('nbc,bf->nfc', xv, w_in2f_v) / math.sqrt(B)
        s = hs[idx_j]
        v = hv[idx_j]
        ys = Yr_ij[:, 0]
        yv = Yr_ij[:, 1:4]
        t_s1 = s * ys[:, None]
        t_s2 = jnp.einsum('efc,ec->ef', v, yv) * IS3
        t_v1 = s[:, :, None] * yv[:, None, :]
        t_v2 = v * ys[:, None, None]
        t_pv = jnp.cross(v, yv[:, None, :]) * IS2
        ax, ay, az = (v[..., 0], v[..., 1], v[..., 2])
        bx, by, bz = (yv[:, None, 0:1], yv[:, None, 1:2], yv[:, None, 2:3])
        bx, by, bz = (bx[..., 0], by[..., 0], bz[..., 0])
        t_q = jnp.stack([(ax * by + ay * bx) * IS2, (ay * bz + az * by) * IS2, (2.0 * az * bz - ax * bx - ay * by) * IS6, (ax * bz + az * bx) * IS2, (ax * bx - ay * by) * IS2], axis=-1)
        h = ssp(f_ij @ W1 + b1)
        Wij = (h @ W2 + b2) * rcut_ij[:, None]
        Wf = Wij.reshape(-1, F, 6)
        edge = jnp.concatenate([(t_s1 * Wf[..., 0])[..., None], (t_s2 * Wf[..., 1])[..., None], t_v1 * Wf[..., 2:3], t_v2 * Wf[..., 3:4], t_pv * Wf[..., 4:5], t_q * Wf[..., 5:6]], axis=-1)
        agg = jax.ops.segment_sum(edge.reshape(edge.shape[0], -1), idx_i, num_segments=n).reshape(n, F, 16)
        s_in = jnp.concatenate([agg[..., 0], agg[..., 1]], axis=1)
        v_in = jnp.concatenate([agg[..., 2:5], agg[..., 5:8]], axis=1)
        os1 = s_in @ w_f2o1_s / math.sqrt(2 * F)
        ov1 = jnp.einsum('nmc,mb->nbc', v_in, w_f2o1_v) / math.sqrt(2 * F)
        os1 = ssp(os1)
        os2 = os1 @ w_f2o2_s / math.sqrt(B)
        ov2 = jnp.einsum('nbc,bd->ndc', ov1, w_f2o2_v) / math.sqrt(B)
        return jnp.concatenate([os2, ov2.reshape(n, -1)], axis=-1)
    edge_index = jnp.stack([src, dst])
    h = jnp.maximum(_layernorm(x, axis=-1), 0.0)
    x = x + _L0_gnn_ref(h, edge_index, L0_gnn_weight, L0_gnn_bias)
    h = jnp.maximum(_layernorm(x, axis=-1), 0.0)
    x = x + _L1_gnn_ref(h, src, dst, edge_attr_20, edge_weight, edge_attr_4, L1_gnn_w_in2f_s, L1_gnn_w_in2f_v, L1_gnn_W1, L1_gnn_b1, L1_gnn_W2, L1_gnn_b2, L1_gnn_w_f2o1_s, L1_gnn_w_f2o1_v, L1_gnn_w_f2o2_s, L1_gnn_w_f2o2_v)
    return x

_drawn_inputs = setup_inputs


def setup_inputs(seed=0):
    import zlib

    import numpy as np

    out = dict(_drawn_inputs(seed))
    spreads = {'L0_gnn_bias': (0.0, 0.72), 'L1_gnn_b1': (0.0, 0.8), 'L1_gnn_b2': (0.0, 0.457)}
    factors = {}
    for name, (base, spread) in spreads.items():
        noise = np.random.default_rng([zlib.crc32(name.encode()), seed]).standard_normal(out[name].shape)
        drawn = base * np.exp(spread * noise) if base else spread * noise
        out[name] = jnp.asarray(drawn.astype(out[name].dtype))
    for name, factor in factors.items():
        out[name] = (out[name] * factor).astype(out[name].dtype)
    return out
```

```python
from contextlib import ExitStack
import math

import concourse.bass as bass
from concourse import mybir

P = 128
F32 = mybir.dt.float32
F32R = mybir.dt.float32r
BF16 = mybir.dt.bfloat16
I32 = mybir.dt.int32
ALU = mybir.AluOpType
ACT = mybir.ActivationFunctionType

NODES = 256
FEAT = 512
EDGES = 4096
B = FEAT // 4
F = 32
RADIAL = 20
NCH = NODES // P
KCH = FEAT // P
GROUPS = 4
CHUNKS = EDGES // (GROUPS * P)
TILES = GROUPS * CHUNKS
GLEN = EDGES // GROUPS
LN_EPS = 1e-5
H_SCALE = 1.0 / math.sqrt(B) / math.sqrt(2 * F)
IS3 = 1.0 / math.sqrt(3.0)
OUT_SCALE = 1.0 / math.sqrt(B)

W_IN_S, W_IN_V, W_O1VT, W_O2V, W_O2S, W_O1S, W_B1 = 0, 32, 64, 192, 320, 448, 576
W_PACK = 577
FIL_ORDER = (0, 3, 2, 1)


def gnn_kernel(nc, x, idx, dst_row, edge_cols, radial, w1_diag, w2_rep, b2_row, w_pack, gcn_w, gcn_b, out):
    with ExitStack() as ctx:
        def sb(name, shape, dt=F32):
            return ctx.enter_context(nc.sbuf_tensor(name, shape, dt))

        def sem(name):
            return ctx.enter_context(nc.semaphore(name))

        bank = [ctx.enter_context(nc.psum_tensor(f"bank{i}", [P, 512], F32)) for i in range(8)]
        count_ps = [bank[0][:, 0:NODES], bank[1][:, 0:NODES]]
        h0t_ps = [bank[2][:], bank[3][:]]
        y_ps = [bank[4][:], bank[5][:]]
        z_ps = [bank[6][:], bank[7][:]]
        adj_ps = [bank[2][:, 0:NODES], bank[3][:, 0:NODES]]
        conv_ps = [bank[0][:], bank[1][:]]
        h1t_ps = [bank[2][:], bank[3][:]]
        h_ps = bank[4][:, 0:NCH * P]
        fil_ps = [bank[6][:], bank[7][:]]
        gath_ps = [bank[2][:], bank[3][:]]
        agg_ps = [bank[0][:, 0:NODES], bank[1][:, 0:NODES]]
        wvv_ps = bank[5][:, 0:P]
        os1_ps = bank[4][:, 0:NODES]
        fin_ps = [bank[6][:], bank[7][:]]

        iota_b = sb("iota_b", [P, NODES], BF16)
        node_id = sb("node_id", [P, NCH])
        ident_wide = sb("ident_wide", [P, 3 * P])
        ident = ident_wide[:, P:2 * P]
        ident_b = sb("ident_b", [P, P], BF16)
        ones3 = sb("ones3", [3, P], BF16)
        idx_i = sb("idx_i", [P, 2 * TILES], I32)
        idx_f = sb("idx_f", [P, 2 * TILES])
        dst_low = sb("dst_low", [P, EDGES // 2], I32)
        edge_sb = sb("edge_sb", [P, 5 * TILES])
        w1_sb = sb("w1_sb", [GROUPS * RADIAL, P])
        w2_sb = sb("w2_sb", [P, 4 * F])
        b2_sb = sb("b2_sb", [3, 4 * F])
        wp = sb("wp", [P, W_PACK])
        gw = sb("gw", [P, KCH, FEAT])
        bias_sb = sb("bias_sb", [P, FEAT])
        x_sb = sb("x_sb", [P, NCH, FEAT])
        dst_high = gw[:].rearrange("p k n -> p (k n)").bitcast(I32)
        S = sb("S", [P, TILES, NODES], BF16)
        D = sb("D", [P, TILES, NODES], BF16)
        S_r = sb("S_r", [P, TILES, NODES], F32R)
        DT = sb("DT", [P, NCH, EDGES], BF16)
        stats = sb("stats", [P, NCH, 6])
        mv = sb("mv", [P, NCH, 2])
        negmean = sb("negmean", [P, NCH])
        h0 = sb("h0", [P, NCH, FEAT])
        h0t = sb("h0t", [P, NCH, FEAT])
        count_b = sb("count_b", [P, NCH, NODES], BF16)
        adj = sb("adj", [P, NCH, NODES])
        degs = sb("degs", [P, 2 * NCH])
        roots = sb("roots", [P, 2 * NCH])
        rsq = sb("rsq", [P, 2 * NCH])
        y_s = sb("y_s", [P, NCH, FEAT])
        x1 = sb("x1", [P, NCH, FEAT])
        stats1 = sb("stats1", [P, NCH, 6])
        mv1 = sb("mv1", [P, NCH, 2])
        negmean1 = sb("negmean1", [P, NCH])
        var1 = sb("var1", [P, NCH])
        std1 = sb("std1", [P, NCH])
        rstd1 = sb("rstd1", [P, NCH])
        h1, h1t = h0, h0t
        H = sb("H", [P, NCH, P])
        H_rest = sb("H_rest", [P, NCH, P])
        H_part = sb("H_part", [P, 3, NCH, P], BF16)
        z_abs = sb("z_abs", [P, GLEN])
        radial_sb = z_abs[0:GROUPS * RADIAL]
        z_pos = sb("z_pos", [P, GLEN])
        hid = sb("hid", [P, GLEN])
        w2_diag = sb("w2_diag", [P, GROUPS * 4 * F])
        b2_s = sb("b2_s", [3, 4 * F])
        b2_rest = sb("b2_rest", [3, 2, 4 * F])
        b2_part = sb("b2_part", [3, 3, 4 * F], BF16)
        b2_acc = sb("b2_acc", [3, 2, 4 * F])
        b2_sel = sb("b2_sel", [3, GROUPS, 4 * F], BF16)
        q = sb("q", [P, TILES, 4])
        QW = sb("QW", [P, TILES, 4, 2 * F])
        free = D[:].rearrange("p t n -> p (t n)").bitcast(F32)
        M = free[:, 0:2048].rearrange("p (b t m f) -> p b t m f", b=2, t=GROUPS, m=8)
        dot3 = free[:, 2048:2432].rearrange("p (t c f) -> p t c f", t=GROUPS, c=3)
        dot2 = free[:, 2432:2560].rearrange("p (t f) -> p t f", t=GROUPS)
        out_sb = free[:, 2560:3584].rearrange("p (c f) -> p c f", c=NCH)
        M_hi = sb("M_hi", [P, 2, GROUPS, 8, F], F32R)
        M_lo = sb("M_lo", [P, 2, GROUPS, 8, F], F32R)
        wvv = sb("wvv", [P, 3, P])
        o2s = sb("o2s", [P, P])
        agg_sb = sb("agg_sb", [P, 2, NODES])
        t_abs, t_exp, t_ln, t_pos = (z_pos[:, i * NODES:(i + 1) * NODES] for i in range(4))
        os1 = sb("os1", [P, NODES])

        half = sb("half", [P, 1])
        half_ready = sem("half_ready")

        in_idx, in_x, in_edge, in_radial, in_w1 = map(sem, ("in_idx", "in_x", "in_edge", "in_radial", "in_w1"))
        in_gw, in_pack, in_w2, in_b2, in_bias, in_dst = map(sem, ("in_gw", "in_pack", "in_w2", "in_b2", "in_bias", "in_dst"))
        out_done, in_dst_high = sem("out_done"), sem("in_dst_high")
        iota_ready, ident0, ident_ready, identb_ready = map(sem, ("iota_ready", "ident0", "ident_ready", "identb_ready"))
        idxf_ready, onehots_ready, dt_ready, sr_ready = map(sem, ("idxf_ready", "onehots_ready", "dt_ready", "sr_ready"))
        stats_done, mv_done, negmean_ready, h0_ready = map(sem, ("stats_done", "mv_done", "negmean_ready", "h0_ready"))
        h0t_done, h0t_ready, y_done, counts_done = map(sem, ("h0t_done", "h0t_ready", "y_done", "counts_done"))
        count_ready, adjsum_done, adj_ready, degs_ready = map(sem, ("count_ready", "adjsum_done", "adj_ready", "degs_ready"))
        roots_ready, rsq_ready, ys_ready, conv_done = map(sem, ("roots_ready", "rsq_ready", "ys_ready", "conv_done"))
        xb_ready, x1_ready, stats1_done, mv1_done = map(sem, ("xb_ready", "x1_ready", "stats1_done", "mv1_done"))
        negmean1_ready, var1_ready, std1_ready, rstd1_ready = map(sem, ("negmean1_ready", "var1_ready", "std1_ready", "rstd1_ready"))
        h1_ready, h1t_done, h1t_ready, h_done = map(sem, ("h1_ready", "h1t_done", "h1t_ready", "h_done"))
        H_ready, H_rest_ready, H_part_ready = map(sem, ("H_ready", "H_rest_ready", "H_part_ready"))
        z_done, z_abs_ready, z_exp_ready, z_ln_ready, z_free = map(sem, ("z_done", "z_abs_ready", "z_exp_ready", "z_ln_ready", "z_free"))
        hid_ready, w2_zeroed, w2_ready, b2_step, b2_ready = map(sem, ("hid_ready", "w2_zeroed", "w2_ready", "b2_step", "b2_ready"))
        q_ready, fil_done, qw_ready = map(sem, ("q_ready", "fil_done", "qw_ready"))
        gath_done, gath_used, dot_step, m_ready, mhi_ready, mlo_ready, scat_done = map(
            sem, ("gath_done", "gath_used", "dot_step", "m_ready", "mhi_ready", "mlo_ready", "scat_done"))
        wvv_zeroed, wvv_done, wvv_ready, o2s_ready, agg_ready, os1_done = map(sem, ("wvv_zeroed", "wvv_done", "wvv_ready", "o2s_ready", "agg_ready", "os1_done"))
        t_abs_ready, t_exp_ready, t_ln_ready, t_pos_ready, os1_ready, fin_done, out_ready = map(
            sem, ("t_abs_ready", "t_exp_ready", "t_ln_ready", "t_pos_ready", "os1_ready", "fin_done", "out_ready"))

        x_v = x.rearrange("(c p) f -> p c f", p=P)
        out_v = out.rearrange("(c p) f -> p c f", p=P)
        gw_v = gcn_w.rearrange("(k p) n -> p k n", p=P)

        block = ctx.enter_context(nc.Block())

        @block.sync
        def _(sp):
            sp.dma_start(idx_i[:], idx).then_inc(in_idx, 16)
            sp.dma_start(x_sb[:], x_v).then_inc(in_x, 16)
            sp.dma_start(gw[:, 0:2], gw_v[:, 0:2]).then_inc(in_gw, 16)
            sp.dma_start(gw[:, 2:4], gw_v[:, 2:4]).then_inc(in_gw, 16)
            sp.dma_start(w1_sb[:], w1_diag).then_inc(in_w1, 16)
            sp.dma_start(radial_sb, radial).then_inc(in_radial, 16)
            sp.dma_start(wp[:], w_pack).then_inc(in_pack, 16)
            sp.dma_start(edge_sb[:], edge_cols).then_inc(in_edge, 16)
            sp.dma_start(w2_sb[:], w2_rep).then_inc(in_w2, 16)
            sp.dma_start(b2_sb[:], b2_row.to_broadcast([3, 4 * F])).then_inc(in_b2, 16)
            sp.dma_start(bias_sb[:], gcn_b.to_broadcast([P, FEAT])).then_inc(in_bias, 16)
            sp.dma_start(dst_low[:], dst_row[:, 0:EDGES // 2].to_broadcast([P, EDGES // 2])).then_inc(in_dst, 16)
            sp.wait_ge(y_done, NCH)
            sp.dma_start(dst_high, dst_row[:, EDGES // 2:EDGES].to_broadcast([P, EDGES // 2])).then_inc(in_dst_high, 16)
            for c in range(NCH):
                sp.wait_ge(out_ready, c + 1)
                sp.dma_start(out_v[:, c], out_sb[:, c]).then_inc(out_done, 16)
            sp.wait_ge(out_done, 16 * NCH)

        @block.gpsimd
        def _(pool):
            nc.gpsimd.iota(iota_b[:], [[1, NODES]], base=0, channel_multiplier=0,
                           allow_small_or_imprecise_dtypes=True).then_inc(iota_ready, 1)
            nc.gpsimd.memset(ident_wide[:], 0.0).then_inc(ident0, 1)
            pool.wait_ge(ident0, 1)
            nc.gpsimd.affine_select(out=ident_wide[:], in_=ident_wide[:], compare_op=ALU.not_equal, fill=1.0,
                                    base=P, pattern=[[-1, 3 * P]], channel_multiplier=1).then_inc(ident_ready, 1)
            nc.gpsimd.iota(node_id[:], [[P, NCH]], base=0, channel_multiplier=1,
                           allow_small_or_imprecise_dtypes=True).then_inc(iota_ready, 1)
            pool.wait_ge(ident_ready, 1)
            nc.gpsimd.tensor_copy(ident_b[:], ident).then_inc(identb_ready, 1)
            nc.gpsimd.memset(ones3[:], 1.0).then_inc(b2_ready, 1)
            nc.gpsimd.memset(wvv[:], 0.0).then_inc(wvv_zeroed, 1)
            nc.gpsimd.memset(w2_diag[:], 0.0).then_inc(w2_zeroed, 1)
            pool.wait_ge(w2_zeroed, 1)
            pool.wait_ge(in_w2, 16)
            for g in range(GROUPS):
                rows = slice(F * g, F * g + F)
                col = g * 4 * F
                if g >= 1:
                    pool.wait_ge(w2_ready, 2 * g)
                nc.gpsimd.tensor_copy(w2_diag[rows, col:col + 3 * F], w2_sb[rows, 0:3 * F]).then_inc(w2_ready, 1)
                nc.gpsimd.tensor_scalar(w2_diag[rows, col + 3 * F:col + 4 * F], w2_sb[rows, 3 * F:4 * F], IS3, None,
                                        ALU.mult).then_inc(w2_ready, 1)
            pool.wait_ge(w2_ready, 2 * GROUPS)
            pool.wait_ge(in_edge, 16)
            nc.gpsimd.tensor_tensor(q[:], edge_sb[:, 0:4 * TILES].rearrange("p (t c) -> p t c", c=4),
                                    edge_sb[:, 4 * TILES:5 * TILES, None].to_broadcast([P, TILES, 4]),
                                    ALU.mult).then_inc(q_ready, 1)
            for n in range(2):
                cols = slice(512 * n, 512 * n + 512)
                pool.wait_ge(z_ln_ready, n + 1)
                nc.gpsimd.tensor_tensor(hid[:, cols], z_abs[:, cols], z_pos[:, cols], ALU.add).then_inc(hid_ready, 1)
            pool.wait_ge(in_bias, 16)
            pool.wait_ge(in_x, 16)
            pool.wait_ge(stats_done, NCH)
            pool.wait_ge(h0_ready, NCH)
            nc.gpsimd.tensor_tensor(x_sb[:], x_sb[:], bias_sb[:, None, :].to_broadcast([P, NCH, FEAT]),
                                    ALU.add).then_inc(xb_ready, 1)
            pool.wait_ge(in_pack, 16)
            nc.gpsimd.tensor_scalar(o2s[:], wp[:, W_O2S:W_O2S + P], OUT_SCALE, None, ALU.mult).then_inc(o2s_ready, 1)

        @block.scalar
        def _(act):
            nc.scalar.preload_act_table_set("natural_log_exp_and_others")
            act.wait_ge(negmean_ready, 1)
            for c in range(NCH):
                nc.scalar.activation(h0[:, c], x_sb[:, c], ACT.Relu, bias=negmean[:, c:c + 1]).then_inc(h0_ready, 1)
            for c in range(NCH):
                act.wait_ge(h0t_done, c + 1)
                nc.scalar.copy(h0t[:, c], h0t_ps[c]).then_inc(h0t_ready, 1)
            act.wait_ge(in_pack, 16)
            act.wait_ge(half_ready, 1)
            b1 = wp[:, W_B1:W_B1 + 1]
            for n in range(2):
                cols = slice(512 * n, 512 * n + 512)
                act.wait_ge(z_done, n + 1)
                nc.scalar.activation(z_abs[:, cols], z_ps[n], ACT.Abs, bias=b1).then_inc(z_abs_ready, 1)
                nc.scalar.activation(z_pos[:, cols], z_ps[n], ACT.Relu, bias=b1).then_inc(z_free, 1)
                act.wait_ge(z_abs_ready, n + 1)
                nc.scalar.activation(z_abs[:, cols], z_abs[:, cols], ACT.Exp, scale=-1.0).then_inc(z_exp_ready, 1)
                act.wait_ge(z_exp_ready, n + 1)
                nc.scalar.activation(z_abs[:, cols], z_abs[:, cols], ACT.Ln, bias=half[:], scale=0.5).then_inc(z_ln_ready, 1)
            nc.scalar.preload_act_table_set("sqrt_and_others")
            for k in range(5):
                act.wait_ge(onehots_ready, k + 1)
                nc.scalar.copy(S_r[:, k * GROUPS:(k + 1) * GROUPS], S[:, k * GROUPS:(k + 1) * GROUPS]).then_inc(sr_ready, 1)
            act.wait_ge(degs_ready, 2)
            nc.scalar.activation(roots[:], degs[:], ACT.Sqrt).then_inc(roots_ready, 1)
            act.wait_ge(y_done, 2)
            act.wait_ge(rsq_ready, 1)
            nc.scalar.activation(y_s[:, 1], y_ps[1], ACT.Copy, scale=rsq[:, 3:4]).then_inc(ys_ready, 1)
            act.wait_ge(var1_ready, 1)
            nc.scalar.activation(std1[:], var1[:], ACT.Sqrt).then_inc(std1_ready, 1)
            nc.scalar.preload_act_table_set("natural_log_exp_and_others")
            act.wait_ge(h1t_done, 1)
            nc.scalar.copy(h1t[:, 0], h1t_ps[0]).then_inc(h1t_ready, 1)
            for k in range(5, CHUNKS):
                act.wait_ge(onehots_ready, k + 1)
                nc.scalar.copy(S_r[:, k * GROUPS:(k + 1) * GROUPS], S[:, k * GROUPS:(k + 1) * GROUPS]).then_inc(sr_ready, 1)
            act.wait_ge(wvv_done, 1)
            act.wait_ge(wvv_zeroed, 1)
            nc.scalar.mul(wvv[2 * F:P, 0:3:2], wvv_ps[2 * F:P, None, :].to_broadcast([2 * F, 2, P]),
                          OUT_SCALE).then_inc(wvv_ready, 1)
            nc.scalar.mul(wvv[0:2 * F, 1], wvv_ps[0:2 * F], OUT_SCALE).then_inc(wvv_ready, 1)
            for k in range(CHUNKS):
                act.wait_ge(m_ready, 3 * k + 3)
                if k >= 2:
                    act.wait_ge(scat_done, k - 1)
                nc.scalar.copy(M_hi[:, k % 2], M[:, k % 2]).then_inc(mhi_ready, 1)
            act.wait_ge(scat_done, CHUNKS)
            nc.scalar.copy(agg_sb[:, 0], agg_ps[0]).then_inc(agg_ready, 1)
            act.wait_ge(os1_done, 1)
            nc.scalar.activation(t_abs, os1_ps, ACT.Abs).then_inc(t_abs_ready, 1)
            act.wait_ge(t_abs_ready, 1)
            nc.scalar.activation(t_exp, t_abs, ACT.Exp, scale=-1.0).then_inc(t_exp_ready, 1)
            act.wait_ge(t_exp_ready, 1)
            nc.scalar.activation(t_ln, t_exp, ACT.Ln, bias=half[:], scale=0.5).then_inc(t_ln_ready, 1)

        @block.vector
        def _(dve):
            nc.vector.memset(half[:], 0.5).then_inc(half_ready, 1)
            dve.wait_ge(in_idx, 16)
            nc.vector.tensor_copy(idx_f[:], idx_i[:]).then_inc(idxf_ready, 1)
            dve.wait_ge(in_x, 16)
            for c in range(NCH):
                nc.vector.bn_stats(stats[:, c], x_sb[:, c]).then_inc(stats_done, 1)
            dve.wait_ge(stats_done, NCH)
            for c in range(NCH):
                nc.vector.bn_aggr(mv[:, c], stats[:, c]).then_inc(mv_done, 1)
            dve.wait_ge(mv_done, NCH)
            nc.vector.tensor_scalar(negmean[:], mv[:, :, 0], -1.0, None, ALU.mult).then_inc(negmean_ready, 1)
            dve.wait_ge(idxf_ready, 1)
            dve.wait_ge(iota_ready, 2)
            for k in range(CHUNKS):
                for g in range(GROUPS):
                    t = k * GROUPS + g
                    nc.vector.tensor_scalar(S[:, t], iota_b[:], idx_f[:, t:t + 1], None, ALU.is_equal)
                    last = nc.vector.tensor_scalar(D[:, t], iota_b[:], idx_f[:, TILES + t:TILES + t + 1], None,
                                                   ALU.is_equal)
                last.then_inc(onehots_ready, 1)
            dve.wait_ge(counts_done, 1)
            for c in range(NCH):
                nc.vector.tensor_scalar(count_b[:, c], count_ps[c], 1.0, None, ALU.min).then_inc(count_ready, 1)
            dve.wait_ge(adjsum_done, 1)
            dve.wait_ge(ident_ready, 1)
            for c in range(NCH):
                nc.vector.scalar_tensor_tensor(out=adj[:, c], in0=adj_ps[c], scalar=1.0,
                                               in1=ident_wide[:, P - P * c:3 * P - P * c], op0=ALU.min, op1=ALU.add,
                                               accum_out=degs[:, c:c + 1]).then_inc(adj_ready, 1)
            dve.wait_ge(adj_ready, NCH)
            nc.vector.scalar_tensor_tensor(out=degs[:, NCH:2 * NCH], in0=mv[:, :, 1], scalar=LN_EPS,
                                           in1=degs[:, 0:NCH], op0=ALU.add, op1=ALU.mult).then_inc(degs_ready, 2)
            dve.wait_ge(roots_ready, 1)
            nc.vector.reciprocal(rsq[:], roots[:]).then_inc(rsq_ready, 1)
            dve.wait_ge(rsq_ready, 1)
            dve.wait_ge(y_done, 1)
            nc.vector.tensor_scalar(y_s[:, 0], y_ps[0], rsq[:, 2:3], None, ALU.mult).then_inc(ys_ready, 1)
            dve.wait_ge(in_b2, 16)
            nc.vector.tensor_copy(b2_s[:, 0:3 * F], b2_sb[:, 0:3 * F]).then_inc(b2_step, 1)
            nc.vector.tensor_scalar(b2_s[:, 3 * F:4 * F], b2_sb[:, 3 * F:4 * F], IS3, None, ALU.mult).then_inc(b2_step, 1)
            dve.wait_ge(b2_step, 2)
            nc.vector.tensor_copy(b2_part[:, 0], b2_s[:]).then_inc(b2_step, 1)
            dve.wait_ge(b2_step, 3)
            nc.vector.tensor_tensor(b2_rest[:, 0], b2_s[:], b2_part[:, 0], ALU.subtract).then_inc(b2_step, 1)
            nc.vector.tensor_scalar(b2_acc[:, 0], b2_part[:, 0], ident_wide[0:3, P:P + 1], None, ALU.mult).then_inc(b2_step, 1)
            dve.wait_ge(b2_step, 5)
            nc.vector.tensor_copy(b2_part[:, 1], b2_rest[:, 0]).then_inc(b2_step, 1)
            dve.wait_ge(b2_step, 6)
            nc.vector.tensor_tensor(b2_part[:, 2], b2_rest[:, 0], b2_part[:, 1], ALU.subtract).then_inc(b2_step, 1)
            nc.vector.scalar_tensor_tensor(out=b2_acc[:, 1], in0=b2_part[:, 1], scalar=ident_wide[0:3, P + 1:P + 2],
                                           in1=b2_acc[:, 0], op0=ALU.mult, op1=ALU.add).then_inc(b2_step, 1)
            dve.wait_ge(b2_step, 8)
            nc.vector.scalar_tensor_tensor(out=b2_rest[:, 1], in0=b2_part[:, 2], scalar=ident_wide[0:3, P + 2:P + 3],
                                           in1=b2_acc[:, 1], op0=ALU.mult, op1=ALU.add).then_inc(b2_step, 1)
            dve.wait_ge(b2_step, 9)
            nc.vector.tensor_copy(b2_sel[:], b2_rest[:, 1:2].to_broadcast([3, GROUPS, 4 * F])).then_inc(b2_ready, 1)
            dve.wait_ge(in_dst, 16)
            for c in range(NCH):
                nc.vector.tensor_scalar(DT[:, c, 0:EDGES // 2], dst_low[:], node_id[:, c:c + 1], None,
                                        ALU.is_equal).then_inc(dt_ready, 1)
            dve.wait_ge(xb_ready, 1)
            for c in range(NCH):
                dve.wait_ge(conv_done, c + 1)
                nc.vector.scalar_tensor_tensor(out=x1[:, c], in0=conv_ps[c], scalar=rsq[:, c:c + 1], in1=x_sb[:, c],
                                               op0=ALU.mult, op1=ALU.add).then_inc(x1_ready, 1)
                dve.wait_ge(x1_ready, c + 1)
                nc.vector.bn_stats(stats1[:, c], x1[:, c]).then_inc(stats1_done, 1)
                dve.wait_ge(stats1_done, c + 1)
                nc.vector.bn_aggr(mv1[:, c], stats1[:, c]).then_inc(mv1_done, 1)
                dve.wait_ge(mv1_done, c + 1)
                nc.vector.tensor_scalar(h1[:, c], x1[:, c], mv1[:, c, 0:1], 0.0, ALU.subtract,
                                        ALU.max).then_inc(h1_ready, 1)
            nc.vector.tensor_scalar(var1[:], mv1[:, :, 1], LN_EPS, None, ALU.add).then_inc(var1_ready, 1)
            dve.wait_ge(h1t_done, 2)
            nc.vector.tensor_copy(h1t[:, 1], h1t_ps[1]).then_inc(h1t_ready, 1)
            dve.wait_ge(std1_ready, 1)
            nc.vector.reciprocal(rstd1[:], std1[:]).then_inc(rstd1_ready, 1)
            dve.wait_ge(rstd1_ready, 1)
            dve.wait_ge(h_done, 2)
            for c in range(NCH):
                nc.vector.tensor_scalar(H[:, c], h_ps[:, c * P:(c + 1) * P], rstd1[:, c:c + 1], H_SCALE, ALU.mult,
                                        ALU.mult).then_inc(H_ready, 1)
            dve.wait_ge(H_ready, 2)
            nc.vector.tensor_copy(H_part[:, 0], H[:]).then_inc(H_part_ready, 1)
            dve.wait_ge(H_part_ready, 1)
            nc.vector.tensor_tensor(H_rest[:], H[:], H_part[:, 0], ALU.subtract).then_inc(H_rest_ready, 1)
            dve.wait_ge(H_rest_ready, 1)
            nc.vector.tensor_copy(H_part[:, 1], H_rest[:]).then_inc(H_part_ready, 1)
            dve.wait_ge(H_part_ready, 2)
            nc.vector.tensor_tensor(H_part[:, 2], H_rest[:], H_part[:, 1], ALU.subtract).then_inc(H_part_ready, 1)
            dve.wait_ge(in_dst_high, 16)
            for c in range(NCH):
                nc.vector.tensor_scalar(DT[:, c, EDGES // 2:EDGES], dst_high, node_id[:, c:c + 1], None,
                                        ALU.is_equal).then_inc(dt_ready, 1)

            def filters(k):
                ts = slice(k * GROUPS, (k + 1) * GROUPS)
                fil = fil_ps[k % 2].rearrange("p (t h f) -> p t h f", t=GROUPS, h=2)
                dve.wait_ge(fil_done, k + 1)
                if k == 0:
                    dve.wait_ge(q_ready, 1)
                nc.vector.tensor_tensor(QW[:, ts, 0], fil[:, :, 0], q[:, ts, 0:1].to_broadcast([P, GROUPS, 2 * F]),
                                        ALU.mult).then_inc(qw_ready, 1)
                nc.vector.tensor_tensor(QW[:, ts, 1:4], fil[:, :, 1:2].to_broadcast([P, GROUPS, 3, 2 * F]),
                                        q[:, ts, 1:4, None].to_broadcast([P, GROUPS, 3, 2 * F]),
                                        ALU.mult).then_inc(qw_ready, 1)

            def messages(k):
                ts = slice(k * GROUPS, (k + 1) * GROUPS)
                b = k % 2
                gath = gath_ps[b].rearrange("p (t c f) -> p t c f", t=GROUPS, c=4)
                dve.wait_ge(gath_done, k + 1)
                dve.wait_ge(qw_ready, 2 * k + 2)
                if k >= 2:
                    dve.wait_ge(mlo_ready, k - 1)
                nc.vector.tensor_tensor(dot3, gath[:, :, 1:4], QW[:, ts, 1:4, F:2 * F], ALU.mult).then_inc(dot_step, 1)
                nc.vector.tensor_tensor(M[:, b, :, 0:8:2], gath[:, :, 0:1].to_broadcast([P, GROUPS, 4, F]),
                                        QW[:, ts, :, 0:F], ALU.mult).then_inc(m_ready, 1)
                nc.vector.tensor_tensor(M[:, b, :, 3:8:2], gath[:, :, 1:4],
                                        QW[:, ts, 0:1, F:2 * F].to_broadcast([P, GROUPS, 3, F]),
                                        ALU.mult).then_inc(m_ready, 1)
                dve.wait_ge(dot_step, 2 * k + 1)
                nc.vector.tensor_tensor(dot2, dot3[:, :, 0], dot3[:, :, 1], ALU.add).then_inc(dot_step, 1)
                dve.wait_ge(dot_step, 2 * k + 2)
                nc.vector.tensor_tensor(M[:, b, :, 1], dot2, dot3[:, :, 2], ALU.add).then_inc(m_ready, 1)

            def low_parts(k):
                b = k % 2
                dve.wait_ge(mhi_ready, k + 1)
                if k >= 2:
                    dve.wait_ge(scat_done, k - 1)
                nc.vector.tensor_tensor(M_lo[:, b], M[:, b], M_hi[:, b].bitcast(F32), ALU.subtract).then_inc(mlo_ready, 1)

            for k in range(CHUNKS + 1):
                if k < CHUNKS:
                    filters(k)
                    messages(k)
                if k >= 1:
                    low_parts(k - 1)
            dve.wait_ge(scat_done, CHUNKS)
            nc.vector.tensor_copy(agg_sb[:, 1], agg_ps[1]).then_inc(agg_ready, 1)
            dve.wait_ge(t_abs_ready, 1)
            nc.vector.tensor_scalar(t_pos, os1_ps, 0.0, None, ALU.max).then_inc(t_pos_ready, 1)
            dve.wait_ge(t_pos_ready, 1)
            dve.wait_ge(t_ln_ready, 1)
            nc.vector.tensor_tensor(os1[:], t_ln, t_pos, ALU.add).then_inc(os1_ready, 1)
            for c in range(NCH):
                dve.wait_ge(fin_done, c + 1)
                nc.vector.tensor_tensor(out_sb[:, c, B:FEAT].rearrange("p (d c) -> p d c", c=3),
                                        fin_ps[c][:, B:FEAT].rearrange("p (c d) -> p d c", c=3),
                                        x1[:, c, B:FEAT].rearrange("p (d c) -> p d c", c=3), ALU.add)
                nc.vector.tensor_tensor(out_sb[:, c, 0:B], fin_ps[c][:, 0:B], x1[:, c, 0:B],
                                        ALU.add).then_inc(out_ready, 1)

        @block.tensor
        def _(pe):
            pe.wait_ge(ident_ready, 1)
            for c in range(NCH):
                pe.wait_ge(h0_ready, c + 1)
                for k in range(KCH):
                    last = nc.tensor.transpose(h0t_ps[c][:, k * P:(k + 1) * P], h0[:, c, k * P:(k + 1) * P], ident)
                last.then_inc(h0t_done, 1)
            pe.wait_ge(in_w1, 16)
            pe.wait_ge(in_radial, 16)
            for n in range(2):
                nc.tensor.matmul(z_ps[n], w1_sb[:], radial_sb[:, 512 * n:512 * n + 512], start=True,
                                 stop=True).then_inc(z_done, 1)
            for k in range(CHUNKS):
                pe.wait_ge(onehots_ready, k + 1)
                for g in range(GROUPS):
                    t = k * GROUPS + g
                    for c in range(NCH):
                        last = nc.tensor.matmul(count_ps[c], S[:, t, c * P:(c + 1) * P], D[:, t],
                                                start=t == 0, stop=t == TILES - 1)
            last.then_inc(counts_done, 1)

            def convolve_weights(c):
                pe.wait_ge(h0t_ready, c + 1)
                for k in range(KCH):
                    last = nc.tensor.matmul(y_ps[c], h0t[:, c, k * P:(k + 1) * P], gw[:, k], start=k == 0,
                                            stop=k == KCH - 1)
                last.then_inc(y_done, 1)

            pe.wait_ge(in_gw, 32)
            convolve_weights(0)
            pe.wait_ge(h0t_ready, 2)
            pe.wait_ge(count_ready, 2)
            pe.wait_ge(identb_ready, 1)
            for c in range(NCH):
                nc.tensor.matmul(adj_ps[c], ident_b[:], count_b[:, c], start=True, stop=False)
                for j in range(NCH):
                    last = nc.tensor.matmul(adj_ps[c][:, j * P:(j + 1) * P], count_b[:, j, c * P:(c + 1) * P],
                                            ident_b[:], start=False, stop=j == NCH - 1)
            last.then_inc(adjsum_done, 1)
            convolve_weights(1)
            pe.wait_ge(ys_ready, 2)
            for c in range(NCH):
                for j in range(NCH):
                    last = nc.tensor.matmul(conv_ps[c], adj[:, j, c * P:(c + 1) * P], y_s[:, j], start=j == 0,
                                            stop=j == NCH - 1)
                last.then_inc(conv_done, 1)

            def filter_out(k):
                pe.wait_ge(hid_ready, k // 4 + 1)
                if k == 0:
                    pe.wait_ge(z_free, 2)
                    pe.wait_ge(w2_ready, 2 * GROUPS)
                    pe.wait_ge(b2_ready, 2)
                if k >= 2:
                    pe.wait_ge(qw_ready, 2 * k - 2)
                nc.tensor.matmul(fil_ps[k % 2], hid[:, k * P:(k + 1) * P], w2_diag[:], start=True, stop=False)
                nc.tensor.matmul(fil_ps[k % 2], ones3[:], b2_sel[:].rearrange("p g f -> p (g f)"), start=False,
                                 stop=True).then_inc(fil_done, 1)

            filter_out(0)
            filter_out(1)
            pe.wait_ge(in_pack, 16)
            nc.tensor.matmul(wvv_ps, wp[:, W_O1VT:W_O1VT + P], wp[:, W_O2V:W_O2V + P], start=True,
                             stop=True).then_inc(wvv_done, 1)
            for c in range(NCH):
                pe.wait_ge(h1_ready, c + 1)
                for n in range(4):
                    part = h1[:, c, 0:B] if n == 0 else h1[:, c, B + n - 1:FEAT:3]
                    last = nc.tensor.transpose(h1t_ps[c][:, n * P:(n + 1) * P], part, ident)
                last.then_inc(h1t_done, 1)
            for c in range(NCH):
                pe.wait_ge(h1t_ready, 2)
                for n in range(4):
                    w = wp[:, W_IN_S:W_IN_S + F] if n == 0 else wp[:, W_IN_V:W_IN_V + F]
                    last = nc.tensor.matmul(h_ps[:, c * P + n * F:c * P + (n + 1) * F],
                                            h1t[:, c, n * P:(n + 1) * P], w, start=True, stop=True)
                last.then_inc(h_done, 1)

            def gather(k):
                if k == 0:
                    pe.wait_ge(H_part_ready, 3)
                    pe.wait_ge(dt_ready, 2)
                if k == CHUNKS // 2:
                    pe.wait_ge(dt_ready, 2 * NCH)
                if k >= 2:
                    pe.wait_ge(m_ready, 3 * (k - 1))
                for g in range(GROUPS):
                    t = k * GROUPS + g
                    for n in range(3 * NCH):
                        c, part = n % NCH, n // NCH
                        last = nc.tensor.matmul(gath_ps[k % 2][:, g * P:(g + 1) * P], DT[:, c, t * P:(t + 1) * P],
                                                H_part[:, part, c], start=n == 0, stop=n == 3 * NCH - 1)
                last.then_inc(gath_done, 1)

            def scatter(k):
                pe.wait_ge(mhi_ready, k + 1)
                pe.wait_ge(sr_ready, k + 1)
                for part in (M_hi, M_lo):
                    if part is M_lo:
                        pe.wait_ge(mlo_ready, k + 1)
                    for g in range(GROUPS):
                        t = k * GROUPS + g
                        for half_ in range(2):
                            rows = part[:, k % 2, g, 4 * half_:4 * half_ + 4].rearrange("p m f -> p (m f)")
                            last = nc.tensor.matmul(agg_ps[half_], rows, S_r[:, t],
                                                    start=t == 0 and part is M_hi,
                                                    stop=t == TILES - 1 and part is M_lo)
                last.then_inc(scat_done, 1)

            gather(0)
            for k in range(CHUNKS):
                if k + 2 < CHUNKS:
                    filter_out(k + 2)
                if k + 1 < CHUNKS:
                    gather(k + 1)
                scatter(k)
            pe.wait_ge(agg_ready, 2)
            nc.tensor.matmul(os1_ps, wp[:, W_O1S:W_O1S + P], agg_sb[:, 0], start=True,
                             stop=True).then_inc(os1_done, 1)
            pe.wait_ge(wvv_ready, 2)
            pe.wait_ge(o2s_ready, 1)
            for c in range(NCH):
                nodes = slice(c * P, (c + 1) * P)
                nc.tensor.matmul(fin_ps[c][:, B:2 * B], agg_sb[:, 0, nodes], wvv[:, 0], start=True, stop=True)
                nc.tensor.matmul(fin_ps[c][:, 2 * B:4 * B], agg_sb[:, 1, nodes],
                                 wvv[:, 1:3].rearrange("p d n -> p (d n)"), start=True, stop=True)
            pe.wait_ge(os1_ready, 1)
            for c in range(NCH):
                nc.tensor.matmul(fin_ps[c][:, 0:B], os1[:, c * P:(c + 1) * P], o2s[:], start=True,
                                 stop=True).then_inc(fin_done, 1)


_INS = ["x", "idx", "dst_row", "edge_cols", "radial", "w1_diag", "w2_rep", "b2_row", "w_pack", "gcn_w", "gcn_b"]


def lay_out(i):
    import numpy as np

    def tiles(a):
        a = np.asarray(a)
        a = a.reshape((GROUPS, CHUNKS, P) + a.shape[1:])
        a = np.moveaxis(a, (2, 1, 0), (0, 1, 2))
        return np.ascontiguousarray(a.reshape((P, TILES) + a.shape[3:]))

    src, dst = np.asarray(i["src"]), np.asarray(i["dst"])
    w1 = np.asarray(i["L1_gnn_W1"])
    w1_diag = np.zeros((GROUPS * RADIAL, P), w1.dtype)
    for g in range(GROUPS):
        w1_diag[g * RADIAL:(g + 1) * RADIAL, g * F:(g + 1) * F] = w1
    w2 = np.asarray(i["L1_gnn_W2"]).reshape(F, F, 6)[:, :, list(FIL_ORDER)]
    w2 = w2.transpose(0, 2, 1).reshape(F, 4 * F)
    b2 = np.asarray(i["L1_gnn_b2"]).reshape(F, 6)[:, list(FIL_ORDER)].T.reshape(1, 4 * F)
    pack = np.zeros((P, W_PACK), w1.dtype)
    pack[:, W_IN_S:W_IN_S + F] = i["L1_gnn_w_in2f_s"]
    pack[:, W_IN_V:W_IN_V + F] = i["L1_gnn_w_in2f_v"]
    pack[:, W_O1VT:W_O1VT + P] = np.tile(np.asarray(i["L1_gnn_w_f2o1_v"]).T, (1, 2))
    pack[:, W_O2V:W_O2V + P] = i["L1_gnn_w_f2o2_v"]
    pack[:, W_O2S:W_O2S + P] = i["L1_gnn_w_f2o2_s"]
    pack[0:2 * F, W_O1S:W_O1S + P] = i["L1_gnn_w_f2o1_s"]
    pack[:, W_B1] = np.tile(np.asarray(i["L1_gnn_b1"]), GROUPS)
    return {
        "x": np.asarray(i["x"]),
        "idx": np.concatenate([tiles(src), tiles(dst)], axis=1),
        "dst_row": dst.reshape(GROUPS, CHUNKS, P).transpose(1, 0, 2).reshape(1, EDGES),
        "edge_cols": np.concatenate([tiles(i["edge_attr_4"]).reshape(P, 4 * TILES), tiles(i["edge_weight"])], axis=1),
        "radial": np.asarray(i["edge_attr_20"]).reshape(GROUPS, GLEN, RADIAL).transpose(0, 2, 1).reshape(-1, GLEN),
        "w1_diag": w1_diag,
        "w2_rep": np.tile(w2, (GROUPS, 1)),
        "b2_row": b2,
        "w_pack": pack,
        "gcn_w": np.asarray(i["L0_gnn_weight"]),
        "gcn_b": np.asarray(i["L0_gnn_bias"]).reshape(1, FEAT),
    }


def kernel(**inputs):
    import numpy as np
    import concourse.bacc as bacc
    from concourse.bass_utils import run_bass_kernel_spmd

    nc = bacc.Bacc("TRN2", target_bir_lowering=False, num_devices=1)
    laid = lay_out(inputs)
    arrays, args = {}, []
    for name in _INS:
        a = np.ascontiguousarray(laid[name])
        arrays[f"in_{name}"] = a
        args.append(nc.dram_tensor(f"in_{name}", a.shape, mybir.dt.from_np(a.dtype), kind="ExternalInput").ap())
    out = nc.dram_tensor("out_x", (NODES, FEAT), F32, kind="ExternalOutput").ap()
    gnn_kernel(nc, *args, out)
    r = run_bass_kernel_spmd(nc, [arrays], core_ids=[0])
    return r.results[0]["out_x"]
```

```python
from contextlib import ExitStack
import math

import concourse.bass as bass
from concourse import mybir

P = 128
F32 = mybir.dt.float32
F32R = mybir.dt.float32r
BF16 = mybir.dt.bfloat16
I32 = mybir.dt.int32
ALU = mybir.AluOpType
ACT = mybir.ActivationFunctionType

NODES = 256
FEAT = 512
EDGES = 4096
B = FEAT // 4
F = 32
RADIAL = 20
NCH = NODES // P
KCH = FEAT // P
GROUPS = 4
CHUNKS = EDGES // (GROUPS * P)
TILES = GROUPS * CHUNKS
GLEN = EDGES // GROUPS
LN_EPS = 1e-5
H_SCALE = 1.0 / math.sqrt(B) / math.sqrt(2 * F)
IS3 = 1.0 / math.sqrt(3.0)
OUT_SCALE = 1.0 / math.sqrt(B)
FIL_AHEAD = 4
LO_DVE = 2

W_IN_S, W_IN_V, W_O1VT, W_O2V, W_O2S, W_O1S, W_B1 = 0, 32, 64, 192, 320, 448, 576
W_PACK = 577
FIL_ORDER = (0, 3, 2, 1)


def gnn_kernel(nc, x, idx, dst_row, edge_cols, radial, w1_diag, w2_diag, b2_row, w_pack, gcn_w, gcn_b, out):
    with ExitStack() as ctx:
        def sb(name, shape, dt=F32):
            return ctx.enter_context(nc.sbuf_tensor(name, shape, dt))

        def sem(name):
            return ctx.enter_context(nc.semaphore(name))

        bank = [ctx.enter_context(nc.psum_tensor(f"bank{i}", [P, 512], F32)) for i in range(8)]
        count_ps = [bank[0][:, 0:NODES], bank[1][:, 0:NODES]]
        h0t_ps = [bank[2][:], bank[3][:]]
        y_ps = [bank[4][:], bank[5][:]]
        z_ps = [bank[6][:], bank[7][:]]
        adj_ps = [bank[2][:, 0:NODES], bank[3][:, 0:NODES]]
        conv_ps = [bank[0][:], bank[1][:]]
        h1t_ps = [bank[2][:], bank[3][:]]
        h_ps = bank[4][:, 0:NCH * P]
        fil_ps = [bank[6][:], bank[7][:]]
        gath_ps = [bank[2][:], bank[3][:]]
        agg_ps = [bank[0][:, 0:NODES], bank[1][:, 0:NODES]]
        wvv_ps = bank[5][:, 0:P]
        os1_ps = bank[4][:, 0:NODES]
        fin_ps = [bank[6][:], bank[7][:]]
        os2_ps = bank[5][:, 0:NODES]

        iota_b = sb("iota_b", [P, NODES], BF16)
        node_id = sb("node_id", [P, NCH])
        ident_wide = sb("ident_wide", [P, 3 * P])
        ident = ident_wide[:, P:2 * P]
        ident_b = sb("ident_b", [P, P], BF16)
        ones3 = sb("ones3", [3, P], BF16)
        idx_i = sb("idx_i", [P, 2 * TILES], I32)
        idx_b = sb("idx_b", [P, 2 * TILES, 2], BF16)
        edge_sb = sb("edge_sb", [P, 5 * TILES])
        w1_sb = sb("w1_sb", [GROUPS * RADIAL, P])
        b2_sb = sb("b2_sb", [3, 4 * F])
        wp = sb("wp", [P, W_PACK])
        gw_hi = sb("gw_hi", [P, KCH, FEAT], F32R)
        gw_lo = sb("gw_lo", [P, KCH, FEAT], F32R)
        bias_sb = sb("bias_sb", [P, FEAT])
        x_sb = sb("x_sb", [P, NCH, FEAT])
        S = sb("S", [P, TILES, NODES], BF16)
        D = sb("D", [P, TILES, NODES], BF16)
        S_r = sb("S_r", [P, TILES, NODES], F32R)
        DT = sb("DT", [P, NCH, EDGES], BF16)
        stats = sb("stats", [P, NCH, 6])
        mv = sb("mv", [P, NCH, 2])
        negmean = sb("negmean", [P, NCH])
        h0 = sb("h0", [P, NCH, FEAT])
        h0t_hi = sb("h0t_hi", [P, NCH, FEAT], F32R)
        h0t_lo = sb("h0t_lo", [P, NCH, FEAT], F32R)
        count_b = sb("count_b", [P, NCH, NODES], BF16)
        adj = sb("adj", [P, NCH, NODES], F32R)
        degs = sb("degs", [P, 2 * NCH])
        roots = sb("roots", [P, 2 * NCH])
        rsq = sb("rsq", [P, 2 * NCH])
        y_hi = sb("y_hi", [P, NCH, FEAT], F32R)
        y_lo = sb("y_lo", [P, NCH, FEAT], F32R)
        x1 = sb("x1", [P, NCH, FEAT])
        stats1 = sb("stats1", [P, NCH, 6])
        mv1 = sb("mv1", [P, NCH, 2])
        sum1 = sb("sum1", [P, NCH])
        mean1 = sb("mean1", [P, NCH])
        var1 = sb("var1", [P, NCH])
        std1 = sb("std1", [P, NCH])
        rstd1 = sb("rstd1", [P, NCH])
        h1 = h0
        h1t = sb("h1t", [P, NCH, FEAT])
        H = sb("H", [P, NCH, P])
        H_rest = sb("H_rest", [P, NCH, P])
        H_part = sb("H_part", [P, 3, NCH, P], BF16)
        z_abs = sb("z_abs", [P, GLEN])
        radial_sb = z_abs[0:GROUPS * RADIAL]
        z_pos = sb("z_pos", [P, GLEN])
        hid = sb("hid", [P, GLEN])
        w2_sb = sb("w2_sb", [P, GROUPS * 4 * F])
        b2_rest = sb("b2_rest", [3, 4 * F])
        b2_part = sb("b2_part", [3, 3, 4 * F], BF16)
        b2_row_part = sb("b2_row_part", [3, 3, 4 * F], BF16)
        b2_sum = sb("b2_sum", [3, 4 * F])
        b2_sel = sb("b2_sel", [3, GROUPS, 4 * F], BF16)
        q = sb("q", [P, TILES, 4])
        QW = sb("QW", [P, TILES, 4, 2 * F])
        fil_sb = sb("fil_sb", [P, 2, 512])
        early = QW[:].rearrange("p t c f -> p (t c f)")
        gw = early[:, 0:2048].rearrange("p (k n) -> p k n", k=KCH)
        dst_b = early[:, 2048:4096].bitcast(BF16)
        free = D[:].rearrange("p t n -> p (t n)").bitcast(F32)
        M = free[:, 0:2048].rearrange("p (b t m f) -> p b t m f", b=2, t=GROUPS, m=8)
        dot3 = free[:, 2048:2432].rearrange("p (t c f) -> p t c f", t=GROUPS, c=3)
        dot2 = free[:, 2432:2560].rearrange("p (t f) -> p t f", t=GROUPS)
        out_sb = free[:, 2560:3584].rearrange("p (c f) -> p c f", c=NCH)
        M_hi, M_lo = (part[:].rearrange("p k n -> p (k n)").rearrange("p (b t m f) -> p b t m f", b=2, t=GROUPS, m=8)
                      for part in (gw_hi, gw_lo))
        wvv = sb("wvv", [P, 3, P])
        o2s = sb("o2s", [P, P])
        agg_sb = sb("agg_sb", [P, 2, NODES])
        t_abs, t_exp, t_ln, t_pos = (z_pos[:, i * NODES:(i + 1) * NODES] for i in range(4))
        os1 = sb("os1", [P, NODES])

        half = sb("half", [P, 1])
        half_ready = sem("half_ready")

        in_idx, in_x, in_edge, in_radial, in_w1 = map(sem, ("in_idx", "in_x", "in_edge", "in_radial", "in_w1"))
        in_gw, in_gw2, in_pack, in_w2, in_b2, in_bias, in_dst = map(sem, ("in_gw", "in_gw2", "in_pack", "in_w2", "in_b2", "in_bias", "in_dst"))
        out_done = sem("out_done")
        iota_ready, ident0, ident_ready, identb_ready = map(sem, ("iota_ready", "ident0", "ident_ready", "identb_ready"))
        idxb_ready, onehots_ready, dt_ready, sr_ready = map(sem, ("idxb_ready", "onehots_ready", "dt_ready", "sr_ready"))
        stats_done, mv_done, negmean_ready, h0_ready = map(sem, ("stats_done", "mv_done", "negmean_ready", "h0_ready"))
        h0t_done, h0t_ready, h0t_lo_ready, gw_hi_ready, gw_lo_ready, y_done, counts_done = map(sem, ("h0t_done", "h0t_ready", "h0t_lo_ready", "gw_hi_ready", "gw_lo_ready", "y_done", "counts_done"))
        count_ready, adjsum_done, adj_ready, degs_ready = map(sem, ("count_ready", "adjsum_done", "adj_ready", "degs_ready"))
        roots_ready, rsq_ready, yhi_ready, ylo_ready, conv_done = map(sem, ("roots_ready", "rsq_ready", "yhi_ready", "ylo_ready", "conv_done"))
        xb_ready, x1_ready, stats1_done, mv1_done = map(sem, ("xb_ready", "x1_ready", "stats1_done", "mv1_done"))
        var1_ready, std1_ready, rstd1_ready = map(sem, ("var1_ready", "std1_ready", "rstd1_ready"))
        h1_ready, h1t_done, h_done = map(sem, ("h1_ready", "h1t_done", "h_done"))
        h1t_ready = [sem(f"h1t{c}_ready") for c in range(NCH)]
        H_ready, H_rest_ready, H_part_ready = map(sem, ("H_ready", "H_rest_ready", "H_part_ready"))
        z_done, z_abs_ready, z_exp_ready, z_ln_ready, z_free = map(sem, ("z_done", "z_abs_ready", "z_exp_ready", "z_ln_ready", "z_free"))
        hid_ready, b2_step, b2_ready, filsb_ready, sum1_ready, o1s_ready = map(sem, ("hid_ready", "b2_step", "b2_ready", "filsb_ready", "sum1_ready", "o1s_ready"))
        q_ready, fil_done, qw_ready = map(sem, ("q_ready", "fil_done", "qw_ready"))
        gath_done, gath_used, dot_step, m_ready, mhi_ready, mlo_ready, mlo_pool_ready, scat_hi_done, scat_lo_done = map(
            sem, ("gath_done", "gath_used", "dot_step", "m_ready", "mhi_ready", "mlo_ready", "mlo_pool_ready", "scat_hi_done", "scat_lo_done"))
        wvv_zeroed, wvv_done, wvv_ready, o2s_ready, agg_ready, os1_done = map(sem, ("wvv_zeroed", "wvv_done", "wvv_ready", "o2s_ready", "agg_ready", "os1_done"))
        t_abs_ready, t_exp_ready, t_ln_ready, t_pos_ready, os1_ready, fin_done, os2_done, out_ready = map(
            sem, ("t_abs_ready", "t_exp_ready", "t_ln_ready", "t_pos_ready", "os1_ready", "fin_done", "os2_done", "out_ready"))

        x_v = x.rearrange("(c p) f -> p c f", p=P)
        out_v = out.rearrange("(c p) f -> p c f", p=P)
        gw_v = gcn_w.rearrange("(k p) n -> p k n", p=P)

        block = ctx.enter_context(nc.Block())

        @block.sync
        def _(sp):
            sp.dma_start(idx_i[:], idx).then_inc(in_idx, 16)
            sp.dma_start(x_sb[:], x_v).then_inc(in_x, 16)
            sp.dma_start(w1_sb[:], w1_diag).then_inc(in_w1, 16)
            sp.dma_start(radial_sb, radial).then_inc(in_radial, 16)
            sp.dma_start(gw[:, 0:2], gw_v[:, 0:2]).then_inc(in_gw, 16)
            sp.dma_start(gw[:, 2:4], gw_v[:, 2:4]).then_inc(in_gw2, 16)
            sp.dma_start(wp[:], w_pack).then_inc(in_pack, 16)
            sp.dma_start(edge_sb[:], edge_cols).then_inc(in_edge, 16)
            sp.dma_start(b2_sb[:], b2_row.to_broadcast([3, 4 * F])).then_inc(in_b2, 16)
            sp.dma_start(w2_sb[:], w2_diag).then_inc(in_w2, 16)
            sp.dma_start(bias_sb[:], gcn_b.to_broadcast([P, FEAT])).then_inc(in_bias, 16)
            for c in range(NCH):
                sp.wait_ge(out_ready, c + 1)
                sp.dma_start(out_v[:, c, B:FEAT], out_sb[:, c, B:FEAT]).then_inc(out_done, 16)
            sp.wait_ge(out_ready, NCH + 1)
            sp.dma_start(out_v[:, :, 0:B], out_sb[:, :, 0:B]).then_inc(out_done, 16)
            sp.wait_ge(out_done, 16 * (NCH + 1))

        @block.gpsimd
        def _(pool):
            nc.gpsimd.iota(iota_b[:], [[1, NODES]], base=0, channel_multiplier=0,
                           allow_small_or_imprecise_dtypes=True).then_inc(iota_ready, 1)
            nc.gpsimd.dma_start(dst_b, dst_row.to_broadcast([P, EDGES])).then_inc(in_dst, 16)
            nc.gpsimd.memset(ident_wide[:], 0.0).then_inc(ident0, 1)
            pool.wait_ge(ident0, 1)
            nc.gpsimd.affine_select(out=ident_wide[:], in_=ident_wide[:], compare_op=ALU.not_equal, fill=1.0,
                                    base=P, pattern=[[-1, 3 * P]], channel_multiplier=1).then_inc(ident_ready, 1)
            nc.gpsimd.iota(node_id[:], [[P, NCH]], base=0, channel_multiplier=1,
                           allow_small_or_imprecise_dtypes=True).then_inc(iota_ready, 1)
            pool.wait_ge(ident_ready, 1)
            nc.gpsimd.tensor_copy(ident_b[:], ident).then_inc(identb_ready, 1)
            nc.gpsimd.memset(ones3[:], 1.0).then_inc(b2_ready, 1)
            nc.gpsimd.memset(wvv[:], 0.0).then_inc(wvv_zeroed, 1)
            for n, ready in enumerate((in_gw, in_gw2)):
                pool.wait_ge(gw_hi_ready, n + 1)
                nc.gpsimd.tensor_tensor(gw_lo[:, 2 * n:2 * n + 2], gw[:, 2 * n:2 * n + 2],
                                        gw_hi[:, 2 * n:2 * n + 2].bitcast(F32), ALU.subtract).then_inc(gw_lo_ready, 1)
            for n in range(2):
                cols = slice(512 * n, 512 * n + 512)
                pool.wait_ge(z_ln_ready, n + 1)
                nc.gpsimd.tensor_tensor(hid[:, cols], z_abs[:, cols], z_pos[:, cols], ALU.add).then_inc(hid_ready, 1)
            pool.wait_ge(in_bias, 16)
            pool.wait_ge(in_x, 16)
            pool.wait_ge(stats_done, NCH)
            pool.wait_ge(h0_ready, NCH)
            nc.gpsimd.tensor_tensor(x_sb[:], x_sb[:], bias_sb[:, None, :].to_broadcast([P, NCH, FEAT]),
                                    ALU.add).then_inc(xb_ready, 1)
            pool.wait_ge(in_edge, 16)
            nc.gpsimd.tensor_tensor(q[:], edge_sb[:, 0:4 * TILES].rearrange("p (t c) -> p t c", c=4),
                                    edge_sb[:, 4 * TILES:5 * TILES, None].to_broadcast([P, TILES, 4]),
                                    ALU.mult).then_inc(q_ready, 1)
            pool.wait_ge(in_b2, 16)
            pool.wait_ge(q_ready, 1)
            nc.gpsimd.tensor_copy(b2_part[:, 0], b2_sb[:]).then_inc(b2_step, 1)
            pool.wait_ge(b2_step, 1)
            nc.gpsimd.tensor_tensor(b2_rest[:], b2_sb[:], b2_part[:, 0], ALU.subtract).then_inc(b2_step, 1)
            pool.wait_ge(b2_step, 2)
            nc.gpsimd.tensor_copy(b2_part[:, 1], b2_rest[:]).then_inc(b2_step, 1)
            pool.wait_ge(b2_step, 3)
            nc.gpsimd.tensor_tensor(b2_part[:, 2], b2_rest[:], b2_part[:, 1], ALU.subtract).then_inc(b2_step, 1)
            pool.wait_ge(b2_step, 4)
            nc.gpsimd.tensor_tensor(b2_row_part[:], b2_part[:],
                                    ident_wide[0:3, P:P + 3, None].to_broadcast([3, 3, 4 * F]),
                                    ALU.mult).then_inc(b2_step, 1)
            pool.wait_ge(b2_step, 5)
            nc.gpsimd.tensor_tensor(b2_sum[:], b2_row_part[:, 0], b2_row_part[:, 1], ALU.add).then_inc(b2_step, 1)
            pool.wait_ge(b2_step, 6)
            nc.gpsimd.tensor_tensor(b2_sel[:], b2_sum[:, None, :].to_broadcast([3, GROUPS, 4 * F]),
                                    b2_row_part[:, 2:3].to_broadcast([3, GROUPS, 4 * F]), ALU.add).then_inc(b2_ready, 1)
            pool.wait_ge(in_pack, 16)
            pool.wait_ge(b2_ready, 2)
            nc.gpsimd.tensor_scalar(o2s[:], wp[:, W_O2S:W_O2S + P], OUT_SCALE, None, ALU.mult).then_inc(o2s_ready, 1)
            pool.wait_ge(o2s_ready, 1)
            nc.gpsimd.tensor_scalar(wp[F:2 * F, W_O1S:W_O1S + P], wp[F:2 * F, W_O1S:W_O1S + P], IS3, None,
                                    ALU.mult).then_inc(o1s_ready, 1)
            pool.wait_ge(o1s_ready, 1)
            pool.wait_ge(q_ready, 1)
            pool.wait_ge(gw_lo_ready, 2)

            def filters(k):
                ts = slice(k * GROUPS, (k + 1) * GROUPS)
                fil = fil_sb[:, k % 2].rearrange("p (t h f) -> p t h f", t=GROUPS, h=2)
                pool.wait_ge(filsb_ready, k + 1)
                if k == 2:
                    pool.wait_ge(dt_ready, NCH)
                nc.gpsimd.tensor_tensor(QW[:, ts, 0], fil[:, :, 0], q[:, ts, 0:1].to_broadcast([P, GROUPS, 2 * F]),
                                        ALU.mult).then_inc(qw_ready, 1)
                nc.gpsimd.tensor_tensor(QW[:, ts, 1:4], fil[:, :, 1:2].to_broadcast([P, GROUPS, 3, 2 * F]),
                                        q[:, ts, 1:4, None].to_broadcast([P, GROUPS, 3, 2 * F]),
                                        ALU.mult).then_inc(qw_ready, 1)

            for k in range(FIL_AHEAD):
                filters(k)
            for k in range(CHUNKS):
                pool.wait_ge(mhi_ready, k + 1)
                if k >= 2:
                    pool.wait_ge(scat_lo_done, k - 1)
                gs = slice(LO_DVE, GROUPS)
                nc.gpsimd.tensor_tensor(M_lo[:, k % 2, gs], M[:, k % 2, gs], M_hi[:, k % 2, gs].bitcast(F32),
                                        ALU.subtract).then_inc(mlo_pool_ready, 1)
                if k + FIL_AHEAD < CHUNKS:
                    filters(k + FIL_AHEAD)

        @block.scalar
        def _(act):
            nc.scalar.preload_act_table_set("natural_log_exp_and_others")
            act.wait_ge(negmean_ready, 1)
            for c in range(NCH):
                nc.scalar.activation(h0[:, c], x_sb[:, c], ACT.Relu, bias=negmean[:, c:c + 1]).then_inc(h0_ready, 1)
            for c in range(NCH):
                act.wait_ge(h0t_done, c + 1)
                nc.scalar.copy(h0t_hi[:, c], h0t_ps[c]).then_inc(h0t_ready, 1)
            for n, ready in enumerate((in_gw, in_gw2)):
                act.wait_ge(ready, 16)
                nc.scalar.copy(gw_hi[:, 2 * n:2 * n + 2], gw[:, 2 * n:2 * n + 2]).then_inc(gw_hi_ready, 1)
            act.wait_ge(in_pack, 16)
            act.wait_ge(half_ready, 1)
            b1 = wp[:, W_B1:W_B1 + 1]
            for n in range(2):
                cols = slice(512 * n, 512 * n + 512)
                act.wait_ge(z_done, n + 1)
                nc.scalar.activation(z_abs[:, cols], z_ps[n], ACT.Abs, bias=b1).then_inc(z_abs_ready, 1)
                nc.scalar.activation(z_pos[:, cols], z_ps[n], ACT.Relu, bias=b1).then_inc(z_free, 1)
                act.wait_ge(z_abs_ready, n + 1)
                nc.scalar.activation(z_abs[:, cols], z_abs[:, cols], ACT.Exp, scale=-1.0).then_inc(z_exp_ready, 1)
                act.wait_ge(z_exp_ready, n + 1)
                nc.scalar.activation(z_abs[:, cols], z_abs[:, cols], ACT.Ln, bias=half[:], scale=0.5).then_inc(z_ln_ready, 1)
            nc.scalar.preload_act_table_set("sqrt_and_others")
            act.wait_ge(degs_ready, 2)
            nc.scalar.activation(roots[:], degs[:], ACT.Sqrt).then_inc(roots_ready, 1)

            def scatter_onehots(k):
                act.wait_ge(onehots_ready, k + 1)
                nc.scalar.copy(S_r[:, k * GROUPS:(k + 1) * GROUPS], S[:, k * GROUPS:(k + 1) * GROUPS]).then_inc(sr_ready, 1)

            def filters_out(k):
                act.wait_ge(fil_done, k + 1)
                if k >= 2:
                    act.wait_ge(qw_ready, 2 * k - 2)
                nc.scalar.copy(fil_sb[:, k % 2], fil_ps[k % 2]).then_inc(filsb_ready, 1)

            for k in range(2):
                scatter_onehots(k)
            filters_out(0)
            filters_out(1)
            act.wait_ge(h1t_done, 1)
            nc.scalar.copy(h1t[:, 0], h1t_ps[0]).then_inc(h1t_ready[0], 1)
            act.wait_ge(var1_ready, 1)
            nc.scalar.activation(std1[:], var1[:], ACT.Sqrt).then_inc(std1_ready, 1)
            nc.scalar.preload_act_table_set("natural_log_exp_and_others")
            act.wait_ge(wvv_zeroed, 1)
            act.wait_ge(wvv_done, 1)
            nc.scalar.mul(wvv[2 * F:P, 0:3:2], wvv_ps[2 * F:P, None, :].to_broadcast([2 * F, 2, P]),
                          OUT_SCALE).then_inc(wvv_ready, 1)
            nc.scalar.mul(wvv[0:2 * F, 1], wvv_ps[0:2 * F], OUT_SCALE).then_inc(wvv_ready, 1)
            for k in range(2, FIL_AHEAD):
                scatter_onehots(k)
                filters_out(k)
            for k in range(CHUNKS):
                act.wait_ge(m_ready, 3 * k + 3)
                if k >= 2:
                    act.wait_ge(scat_hi_done, k - 1)
                nc.scalar.copy(M_hi[:, k % 2], M[:, k % 2]).then_inc(mhi_ready, 1)
                if k + FIL_AHEAD < CHUNKS:
                    filters_out(k + FIL_AHEAD)
                    scatter_onehots(k + FIL_AHEAD)
            act.wait_ge(scat_lo_done, CHUNKS)
            nc.scalar.copy(agg_sb[:, 0], agg_ps[0]).then_inc(agg_ready, 1)
            act.wait_ge(os1_done, 1)
            nc.scalar.activation(t_abs, os1_ps, ACT.Abs).then_inc(t_abs_ready, 1)
            act.wait_ge(t_abs_ready, 1)
            nc.scalar.activation(t_exp, t_abs, ACT.Exp, scale=-1.0).then_inc(t_exp_ready, 1)
            act.wait_ge(t_exp_ready, 1)
            nc.scalar.activation(t_ln, t_exp, ACT.Ln, bias=half[:], scale=0.5).then_inc(t_ln_ready, 1)

        @block.vector
        def _(dve):
            nc.vector.memset(half[:], 0.5).then_inc(half_ready, 1)
            dve.wait_ge(in_idx, 16)
            nc.vector.tensor_copy(idx_b[:], idx_i[:, :, None].to_broadcast([P, 2 * TILES, 2])).then_inc(idxb_ready, 1)
            dve.wait_ge(idxb_ready, 1)
            dve.wait_ge(iota_ready, 1)

            def onehots(k):
                for side, hot in enumerate((S, D)):
                    first = side * TILES + k * GROUPS
                    last = nc.vector.tensor_tensor(
                        hot[:, k * GROUPS:(k + 1) * GROUPS].rearrange("p t (n two) -> p t n two", two=2),
                        idx_b[:, first:first + GROUPS, None, :].to_broadcast([P, GROUPS, NODES // 2, 2]),
                        iota_b[:, None, :].to_broadcast([P, GROUPS, NODES]).rearrange("p t (n two) -> p t n two", two=2),
                        ALU.is_equal)
                last.then_inc(onehots_ready, 1)

            onehots(0)
            dve.wait_ge(in_x, 16)
            for c in range(NCH):
                nc.vector.bn_stats(stats[:, c], x_sb[:, c]).then_inc(stats_done, 1)
            dve.wait_ge(stats_done, NCH)
            for c in range(NCH):
                nc.vector.bn_aggr(mv[:, c], stats[:, c]).then_inc(mv_done, 1)
            dve.wait_ge(mv_done, NCH)
            nc.vector.tensor_scalar(negmean[:], mv[:, :, 0], -1.0, None, ALU.mult).then_inc(negmean_ready, 1)
            for k in range(1, 5):
                onehots(k)
            for c in range(NCH):
                dve.wait_ge(h0t_ready, c + 1)
                nc.vector.tensor_tensor(h0t_lo[:, c], h0t_ps[c], h0t_hi[:, c].bitcast(F32),
                                        ALU.subtract).then_inc(h0t_lo_ready, 1)
            for k in range(5, CHUNKS):
                onehots(k)
            dve.wait_ge(counts_done, 1)
            for c in range(NCH):
                nc.vector.tensor_scalar(count_b[:, c], count_ps[c], 1.0, None, ALU.min).then_inc(count_ready, 1)
            dve.wait_ge(adjsum_done, 1)
            dve.wait_ge(ident_ready, 1)
            for c in range(NCH):
                nc.vector.scalar_tensor_tensor(out=adj[:, c], in0=adj_ps[c], scalar=1.0,
                                               in1=ident_wide[:, P - P * c:3 * P - P * c], op0=ALU.min, op1=ALU.add,
                                               accum_out=degs[:, c:c + 1]).then_inc(adj_ready, 1)
            dve.wait_ge(adj_ready, NCH)
            nc.vector.scalar_tensor_tensor(out=degs[:, NCH:2 * NCH], in0=mv[:, :, 1], scalar=LN_EPS,
                                           in1=degs[:, 0:NCH], op0=ALU.add, op1=ALU.mult).then_inc(degs_ready, 2)
            dve.wait_ge(in_dst, 16)
            dve.wait_ge(iota_ready, 2)
            nc.vector.tensor_scalar(DT[:, 0], dst_b, node_id[:, 0:1], None, ALU.is_equal).then_inc(dt_ready, 1)
            dve.wait_ge(roots_ready, 1)
            nc.vector.reciprocal(rsq[:], roots[:]).then_inc(rsq_ready, 1)
            dve.wait_ge(rsq_ready, 1)
            for c in range(NCH):
                if c == 1:
                    nc.vector.tensor_scalar(DT[:, 1], dst_b, node_id[:, 1:2], None, ALU.is_equal).then_inc(dt_ready, 1)
                dve.wait_ge(y_done, c + 1)
                scale = rsq[:, NCH + c:NCH + c + 1]
                nc.vector.tensor_scalar(y_hi[:, c], y_ps[c], scale, None, ALU.mult).then_inc(yhi_ready, 1)
                dve.wait_ge(yhi_ready, c + 1)
                nc.vector.scalar_tensor_tensor(out=y_lo[:, c], in0=y_ps[c], scalar=scale,
                                               in1=y_hi[:, c].bitcast(F32), op0=ALU.mult,
                                               op1=ALU.subtract).then_inc(ylo_ready, 1)
            dve.wait_ge(xb_ready, 1)
            for c in range(NCH):
                dve.wait_ge(conv_done, c + 1)
                nc.vector.scalar_tensor_tensor(out=x1[:, c], in0=conv_ps[c], scalar=rsq[:, c:c + 1], in1=x_sb[:, c],
                                               op0=ALU.mult, op1=ALU.add,
                                               accum_out=sum1[:, c:c + 1]).then_inc(x1_ready, 1)
                dve.wait_ge(x1_ready, c + 1)
                nc.vector.tensor_scalar(mean1[:, c:c + 1], sum1[:, c:c + 1], 1.0 / FEAT, None,
                                        ALU.mult).then_inc(sum1_ready, 1)
                dve.wait_ge(sum1_ready, c + 1)
                nc.vector.tensor_scalar(h1[:, c], x1[:, c], mean1[:, c:c + 1], 0.0, ALU.subtract,
                                        ALU.max).then_inc(h1_ready, 1)
            for c in range(NCH):
                if c == 1:
                    dve.wait_ge(h1t_done, 2)
                    nc.vector.tensor_copy(h1t[:, 1], h1t_ps[1]).then_inc(h1t_ready[1], 1)
                nc.vector.bn_stats(stats1[:, c], x1[:, c]).then_inc(stats1_done, 1)
            dve.wait_ge(stats1_done, NCH)
            for c in range(NCH):
                nc.vector.bn_aggr(mv1[:, c], stats1[:, c]).then_inc(mv1_done, 1)
            dve.wait_ge(mv1_done, NCH)
            nc.vector.tensor_scalar(var1[:], mv1[:, :, 1], LN_EPS, None, ALU.add).then_inc(var1_ready, 1)
            dve.wait_ge(std1_ready, 1)
            nc.vector.reciprocal(rstd1[:], std1[:]).then_inc(rstd1_ready, 1)
            dve.wait_ge(rstd1_ready, 1)
            dve.wait_ge(h_done, 2)
            for c in range(NCH):
                nc.vector.tensor_scalar(H[:, c], h_ps[:, c * P:(c + 1) * P], rstd1[:, c:c + 1], H_SCALE, ALU.mult,
                                        ALU.mult).then_inc(H_ready, 1)
            dve.wait_ge(H_ready, 2)
            nc.vector.tensor_copy(H_part[:, 0], H[:]).then_inc(H_part_ready, 1)
            dve.wait_ge(H_part_ready, 1)
            nc.vector.tensor_tensor(H_rest[:], H[:], H_part[:, 0], ALU.subtract).then_inc(H_rest_ready, 1)
            dve.wait_ge(H_rest_ready, 1)
            nc.vector.tensor_copy(H_part[:, 1], H_rest[:]).then_inc(H_part_ready, 1)
            dve.wait_ge(H_part_ready, 2)
            nc.vector.tensor_tensor(H_part[:, 2], H_rest[:], H_part[:, 1], ALU.subtract).then_inc(H_part_ready, 1)

            def messages(k):
                ts = slice(k * GROUPS, (k + 1) * GROUPS)
                b = k % 2
                gath = gath_ps[b].rearrange("p (t c f) -> p t c f", t=GROUPS, c=4)
                dve.wait_ge(gath_done, k + 1)
                dve.wait_ge(qw_ready, 2 * k + 2)
                if k >= 2:
                    dve.wait_ge(mlo_ready, k - 1)
                    dve.wait_ge(mlo_pool_ready, k - 1)
                if k >= 1:
                    dve.wait_ge(m_ready, 3 * k)
                nc.vector.tensor_tensor(dot3, gath[:, :, 1:4], QW[:, ts, 1:4, F:2 * F], ALU.mult).then_inc(dot_step, 1)
                nc.vector.tensor_tensor(M[:, b, :, 0:8:2], gath[:, :, 0:1].to_broadcast([P, GROUPS, 4, F]),
                                        QW[:, ts, :, 0:F], ALU.mult).then_inc(m_ready, 1)
                nc.vector.tensor_tensor(M[:, b, :, 3:8:2], gath[:, :, 1:4],
                                        QW[:, ts, 0:1, F:2 * F].to_broadcast([P, GROUPS, 3, F]),
                                        ALU.mult).then_inc(m_ready, 1)
                dve.wait_ge(dot_step, 2 * k + 1)
                nc.vector.tensor_tensor(dot2, dot3[:, :, 0], dot3[:, :, 1], ALU.add).then_inc(dot_step, 1)
                dve.wait_ge(dot_step, 2 * k + 2)
                nc.vector.tensor_tensor(M[:, b, :, 1], dot2, dot3[:, :, 2], ALU.add).then_inc(m_ready, 1)

            def low_parts(k):
                b = k % 2
                dve.wait_ge(mhi_ready, k + 1)
                if k >= 2:
                    dve.wait_ge(scat_lo_done, k - 1)
                gs = slice(0, LO_DVE)
                nc.vector.tensor_tensor(M_lo[:, b, gs], M[:, b, gs], M_hi[:, b, gs].bitcast(F32),
                                        ALU.subtract).then_inc(mlo_ready, 1)

            for k in range(CHUNKS + 1):
                if k < CHUNKS:
                    messages(k)
                if k >= 1:
                    low_parts(k - 1)
            dve.wait_ge(scat_lo_done, CHUNKS)
            nc.vector.tensor_copy(agg_sb[:, 1], agg_ps[1]).then_inc(agg_ready, 1)
            dve.wait_ge(t_abs_ready, 1)
            nc.vector.tensor_scalar(t_pos, os1_ps, 0.0, None, ALU.max).then_inc(t_pos_ready, 1)
            dve.wait_ge(t_pos_ready, 1)
            dve.wait_ge(t_ln_ready, 1)
            nc.vector.tensor_tensor(os1[:], t_ln, t_pos, ALU.add).then_inc(os1_ready, 1)
            for c in range(NCH):
                dve.wait_ge(fin_done, c + 1)
                nc.vector.tensor_tensor(out_sb[:, c, B:FEAT].rearrange("p (d c) -> p d c", c=3),
                                        fin_ps[c][:, B:FEAT].rearrange("p (c d) -> p d c", c=3),
                                        x1[:, c, B:FEAT].rearrange("p (d c) -> p d c", c=3),
                                        ALU.add).then_inc(out_ready, 1)
            dve.wait_ge(os2_done, 1)
            nc.vector.tensor_tensor(out_sb[:, :, 0:B], os2_ps.rearrange("p (c d) -> p c d", c=NCH), x1[:, :, 0:B],
                                    ALU.add).then_inc(out_ready, 1)

        @block.tensor
        def _(pe):
            def count(k):
                pe.wait_ge(onehots_ready, k + 1)
                for g in range(GROUPS):
                    t = k * GROUPS + g
                    for c in range(NCH):
                        last = nc.tensor.matmul(count_ps[c], S[:, t, c * P:(c + 1) * P], D[:, t],
                                                start=t == 0, stop=t == TILES - 1)
                if k == CHUNKS - 1:
                    last.then_inc(counts_done, 1)

            count(0)
            pe.wait_ge(in_w1, 16)
            pe.wait_ge(in_radial, 16)
            for n in range(2):
                nc.tensor.matmul(z_ps[n], w1_sb[:], radial_sb[:, 512 * n:512 * n + 512], start=True,
                                 stop=True).then_inc(z_done, 1)
            pe.wait_ge(ident_ready, 1)
            for c in range(NCH):
                pe.wait_ge(h0_ready, c + 1)
                for k in range(KCH):
                    last = nc.tensor.transpose(h0t_ps[c][:, k * P:(k + 1) * P], h0[:, c, k * P:(k + 1) * P], ident)
                last.then_inc(h0t_done, 1)
            for k in range(1, CHUNKS):
                count(k)

            def convolve_weights(c):
                pe.wait_ge(h0t_ready, c + 1)
                n = 0
                for a, b in ((h0t_hi, gw_hi), (h0t_lo, gw_hi), (h0t_hi, gw_lo)):
                    if a is h0t_hi:
                        pe.wait_ge(gw_hi_ready if b is gw_hi else gw_lo_ready, 2)
                    else:
                        pe.wait_ge(h0t_lo_ready, c + 1)
                    for k in range(KCH):
                        last = nc.tensor.matmul(y_ps[c], a[:, c, k * P:(k + 1) * P], b[:, k], start=n == 0,
                                                stop=n == 3 * KCH - 1)
                        n += 1
                last.then_inc(y_done, 1)

            convolve_weights(0)
            pe.wait_ge(h0t_lo_ready, 2)
            pe.wait_ge(count_ready, 2)
            pe.wait_ge(identb_ready, 1)
            for c in range(NCH):
                nc.tensor.matmul(adj_ps[c], ident_b[:], count_b[:, c], start=True, stop=False)
                for j in range(NCH):
                    last = nc.tensor.matmul(adj_ps[c][:, j * P:(j + 1) * P], count_b[:, j, c * P:(c + 1) * P],
                                            ident_b[:], start=False, stop=j == NCH - 1)
            last.then_inc(adjsum_done, 1)
            convolve_weights(1)
            n = 0
            for j in range(NCH):
                for part in (y_hi, y_lo):
                    pe.wait_ge(yhi_ready if part is y_hi else ylo_ready, j + 1)
                    for c in range(NCH):
                        last = nc.tensor.matmul(conv_ps[c], adj[:, j, c * P:(c + 1) * P], part[:, j], start=n == 0,
                                                stop=n == 2 * NCH - 1)
                        if n == 2 * NCH - 1:
                            last.then_inc(conv_done, 1)
                    n += 1

            def filter_out(k):
                pe.wait_ge(hid_ready, k // 4 + 1)
                if k == 0:
                    pe.wait_ge(z_free, 2)
                    pe.wait_ge(in_w2, 16)
                    pe.wait_ge(b2_ready, 2)
                if k >= 2:
                    pe.wait_ge(filsb_ready, k - 1)
                nc.tensor.matmul(fil_ps[k % 2], hid[:, k * P:(k + 1) * P], w2_sb[:], start=True, stop=False)
                nc.tensor.matmul(fil_ps[k % 2], ones3[:], b2_sel[:].rearrange("p g f -> p (g f)"), start=False,
                                 stop=True).then_inc(fil_done, 1)

            for k in range(2):
                filter_out(k)
            pe.wait_ge(in_pack, 16)
            pe.wait_ge(ylo_ready, 2)
            nc.tensor.matmul(wvv_ps, wp[:, W_O1VT:W_O1VT + P], wp[:, W_O2V:W_O2V + P], start=True,
                             stop=True).then_inc(wvv_done, 1)
            for c in range(NCH):
                pe.wait_ge(h1_ready, c + 1)
                for n in range(4):
                    part = h1[:, c, 0:B] if n == 0 else h1[:, c, B + n - 1:FEAT:3]
                    last = nc.tensor.transpose(h1t_ps[c][:, n * P:(n + 1) * P], part, ident)
                last.then_inc(h1t_done, 1)
            pe.wait_ge(ylo_ready, 2)
            for c in range(NCH):
                pe.wait_ge(h1t_ready[c], 1)
                for n in range(4):
                    w = wp[:, W_IN_S:W_IN_S + F] if n == 0 else wp[:, W_IN_V:W_IN_V + F]
                    last = nc.tensor.matmul(h_ps[:, c * P + n * F:c * P + (n + 1) * F],
                                            h1t[:, c, n * P:(n + 1) * P], w, start=True, stop=True)
                last.then_inc(h_done, 1)
            for k in range(2, FIL_AHEAD):
                filter_out(k)

            def gather(k):
                if k == 0:
                    pe.wait_ge(H_part_ready, 3)
                    pe.wait_ge(dt_ready, 2)
                if k >= 2:
                    pe.wait_ge(m_ready, 3 * (k - 1))
                for g in range(GROUPS):
                    t = k * GROUPS + g
                    for n in range(3 * NCH):
                        c, part = n % NCH, n // NCH
                        last = nc.tensor.matmul(gath_ps[k % 2][:, g * P:(g + 1) * P], DT[:, c, t * P:(t + 1) * P],
                                                H_part[:, part, c], start=n == 0, stop=n == 3 * NCH - 1)
                last.then_inc(gath_done, 1)

            def scatter(k, part):
                if part is M_hi:
                    pe.wait_ge(mhi_ready, k + 1)
                    pe.wait_ge(sr_ready, k + 1)
                else:
                    pe.wait_ge(mlo_ready, k + 1)
                    pe.wait_ge(mlo_pool_ready, k + 1)
                for g in range(GROUPS):
                    t = k * GROUPS + g
                    for half_ in range(2):
                        rows = part[:, k % 2, g, 4 * half_:4 * half_ + 4].rearrange("p m f -> p (m f)")
                        last = nc.tensor.matmul(agg_ps[half_], rows, S_r[:, t],
                                                start=t == 0 and part is M_hi,
                                                stop=t == TILES - 1 and part is M_lo)
                last.then_inc(scat_hi_done if part is M_hi else scat_lo_done, 1)

            gather(0)
            gather(1)
            for k in range(CHUNKS):
                if k + FIL_AHEAD < CHUNKS:
                    filter_out(k + FIL_AHEAD)
                if k + 2 < CHUNKS:
                    gather(k + 2)
                if k >= 1:
                    scatter(k - 1, M_lo)
                scatter(k, M_hi)
            scatter(CHUNKS - 1, M_lo)
            pe.wait_ge(agg_ready, 2)
            pe.wait_ge(o1s_ready, 1)
            nc.tensor.matmul(os1_ps, wp[:, W_O1S:W_O1S + P], agg_sb[:, 0], start=True,
                             stop=True).then_inc(os1_done, 1)
            pe.wait_ge(wvv_ready, 2)
            pe.wait_ge(o2s_ready, 1)
            for c in range(NCH):
                nodes = slice(c * P, (c + 1) * P)
                nc.tensor.matmul(fin_ps[c][:, B:2 * B], agg_sb[:, 0, nodes], wvv[:, 0], start=True, stop=True)
                nc.tensor.matmul(fin_ps[c][:, 2 * B:4 * B], agg_sb[:, 1, nodes],
                                 wvv[:, 1:3].rearrange("p d n -> p (d n)"), start=True,
                                 stop=True).then_inc(fin_done, 1)
            pe.wait_ge(os1_ready, 1)
            for c in range(NCH):
                last = nc.tensor.matmul(os2_ps[:, c * P:(c + 1) * P], os1[:, c * P:(c + 1) * P], o2s[:], start=True,
                                        stop=True)
            last.then_inc(os2_done, 1)


_INS = ["x", "idx", "dst_row", "edge_cols", "radial", "w1_diag", "w2_diag", "b2_row", "w_pack", "gcn_w", "gcn_b"]


def lay_out(i):
    import numpy as np

    def tiles(a):
        a = np.asarray(a)
        a = a.reshape((GROUPS, CHUNKS, P) + a.shape[1:])
        a = np.moveaxis(a, (2, 1, 0), (0, 1, 2))
        return np.ascontiguousarray(a.reshape((P, TILES) + a.shape[3:]))

    src, dst = np.asarray(i["src"]), np.asarray(i["dst"])
    w1 = np.asarray(i["L1_gnn_W1"])
    w1_diag = np.zeros((GROUPS * RADIAL, P), w1.dtype)
    for g in range(GROUPS):
        w1_diag[g * RADIAL:(g + 1) * RADIAL, g * F:(g + 1) * F] = w1
    w2 = np.asarray(i["L1_gnn_W2"]).reshape(F, F, 6)[:, :, list(FIL_ORDER)]
    w2 = w2.transpose(0, 2, 1).reshape(F, 4 * F)
    w2_diag = np.zeros((P, GROUPS * 4 * F), w2.dtype)
    for g in range(GROUPS):
        w2_diag[g * F:(g + 1) * F, g * 4 * F:(g + 1) * 4 * F] = w2
    b2 = np.asarray(i["L1_gnn_b2"]).reshape(F, 6)[:, list(FIL_ORDER)].T.reshape(1, 4 * F)
    pack = np.zeros((P, W_PACK), w1.dtype)
    pack[:, W_IN_S:W_IN_S + F] = i["L1_gnn_w_in2f_s"]
    pack[:, W_IN_V:W_IN_V + F] = i["L1_gnn_w_in2f_v"]
    pack[:, W_O1VT:W_O1VT + P] = np.tile(np.asarray(i["L1_gnn_w_f2o1_v"]).T, (1, 2))
    pack[:, W_O2V:W_O2V + P] = i["L1_gnn_w_f2o2_v"]
    pack[:, W_O2S:W_O2S + P] = i["L1_gnn_w_f2o2_s"]
    pack[0:2 * F, W_O1S:W_O1S + P] = i["L1_gnn_w_f2o1_s"]
    pack[:, W_B1] = np.tile(np.asarray(i["L1_gnn_b1"]), GROUPS)
    return {
        "x": np.asarray(i["x"]),
        "idx": np.concatenate([tiles(src), tiles(dst)], axis=1),
        "dst_row": dst.reshape(GROUPS, CHUNKS, P).transpose(1, 0, 2).reshape(1, EDGES),
        "edge_cols": np.concatenate([tiles(i["edge_attr_4"]).reshape(P, 4 * TILES), tiles(i["edge_weight"])], axis=1),
        "radial": np.asarray(i["edge_attr_20"]).reshape(GROUPS, GLEN, RADIAL).transpose(0, 2, 1).reshape(-1, GLEN),
        "w1_diag": w1_diag,
        "w2_diag": w2_diag,
        "b2_row": b2,
        "w_pack": pack,
        "gcn_w": np.asarray(i["L0_gnn_weight"]),
        "gcn_b": np.asarray(i["L0_gnn_bias"]).reshape(1, FEAT),
    }


def kernel(**inputs):
    import numpy as np
    import concourse.bacc as bacc
    from concourse.bass_utils import run_bass_kernel_spmd

    nc = bacc.Bacc("TRN2", target_bir_lowering=False, num_devices=1)
    laid = lay_out(inputs)
    arrays, args = {}, []
    for name in _INS:
        a = np.ascontiguousarray(laid[name])
        arrays[f"in_{name}"] = a
        args.append(nc.dram_tensor(f"in_{name}", a.shape, mybir.dt.from_np(a.dtype), kind="ExternalInput").ap())
    out = nc.dram_tensor("out_x", (NODES, FEAT), F32, kind="ExternalOutput").ap()
    gnn_kernel(nc, *args, out)
    r = run_bass_kernel_spmd(nc, [arrays], core_ids=[0])
    return r.results[0]["out_x"]
```

```python
from contextlib import ExitStack
import math

from concourse import mybir

P = 128
F32 = mybir.dt.float32
F32R = mybir.dt.float32r
BF16 = mybir.dt.bfloat16
I32 = mybir.dt.int32
ALU = mybir.AluOpType
ACT = mybir.ActivationFunctionType

NODES = 256
FEAT = 512
EDGES = 4096
B = FEAT // 4
F = 32
RADIAL = 20
NCH = NODES // P
KCH = FEAT // P
GROUPS = 4
CHUNKS = EDGES // (GROUPS * P)
TILES = GROUPS * CHUNKS
GLEN = EDGES // GROUPS
LN_EPS = 1e-5
H_SCALE = 1.0 / math.sqrt(B) / math.sqrt(2 * F)
IS3 = 1.0 / math.sqrt(3.0)
OUT_SCALE = 1.0 / math.sqrt(B)
WARM_UP = 14
LO_DVE = [2, 2, 2, 2, 1, 1, 1, 3]

W_IN_S, W_IN_V, W_O1VT, W_O2V, W_O2S, W_O1S = 0, 32, 64, 192, 320, 448
W_PACK = 576
FIL_ORDER = (0, 3, 2, 1)


def gnn_kernel(nc, x, idx, dst_row, edge_cols, radial, w1_diag, w2_diag, b2_rows, w_pack, gcn_w, gcn_b, out):
    with ExitStack() as ctx:
        def sb(name, shape, dt=F32):
            return ctx.enter_context(nc.sbuf_tensor(name, shape, dt))

        def sems(names):
            return [ctx.enter_context(nc.semaphore(name)) for name in names.split()]

        bank = [ctx.enter_context(nc.psum_tensor(f"bank{i}", [P, 512], F32)) for i in range(8)]
        count_ps = [bank[0][:, 0:NODES], bank[1][:, 0:NODES]]
        h0t_ps = [bank[2][:], bank[3][:]]
        y_ps = [bank[4][:], bank[5][:]]
        z_ps = [bank[6][:], bank[7][:]]
        adj_ps = [bank[2][:, 0:NODES], bank[3][:, 0:NODES]]
        conv_ps = [bank[0][:], bank[1][:]]
        h1t_ps = [bank[2][:], bank[3][:]]
        h_ps = [bank[4][:, 0:P], bank[0][:, 0:P]]
        fil_ps = [bank[6][:], bank[7][:]]
        gath_ps = [bank[2][:], bank[3][:]]
        agg_ps = [bank[0][:, 0:NODES], bank[1][:, 0:NODES]]
        wvv_ps = bank[5][:, 0:P]
        os1_ps = bank[4][:, 0:NODES]
        fin_ps = [bank[6][:], bank[7][:]]
        os2_ps = [bank[5][:, 0:P], bank[2][:, 0:P]]

        iota_b = sb("iota_b", [P, NODES], BF16)
        node_id = sb("node_id", [P, NCH])
        ident_wide = sb("ident_wide", [P, 3 * P])
        ident = ident_wide[:, P:2 * P]
        ident_b = sb("ident_b", [P, P], BF16)
        sign_f = sb("sign_f", [2, P])
        sign = sb("sign", [2, P], F32R)
        idx_i = sb("idx_i", [P, 2 * TILES], I32)
        idx_b = sb("idx_b", [P, 2 * TILES, 2], BF16)
        last_src = sb("last_src", [P, GROUPS])
        edge_sb = sb("edge_sb", [P, 5 * TILES + 1])
        w1_sb = sb("w1_sb", [GROUPS * RADIAL, P])
        b2_sb = sb("b2_sb", [2, 2, 4 * F])
        wp = sb("wp", [P, W_PACK])
        gw_hi = sb("gw_hi", [P, KCH, FEAT], F32R)
        gw_lo = sb("gw_lo", [P, KCH, FEAT], F32R)
        bias_sb = sb("bias_sb", [P, FEAT])
        x_sb = sb("x_sb", [P, NCH, FEAT])
        S = sb("S", [P, TILES, NODES], BF16)
        D = sb("D", [P, TILES, NODES], BF16)
        S_r = sb("S_r", [P, TILES, NODES], F32R)
        DT = sb("DT", [P, NCH, EDGES], BF16)
        stats = sb("stats", [P, NCH, 6])
        mv = sb("mv", [P, NCH, 2])
        negmean = sb("negmean", [P, NCH])
        h0 = sb("h0", [P, NCH, FEAT])
        h0t_hi = sb("h0t_hi", [P, NCH, FEAT], F32R)
        h0t_lo = sb("h0t_lo", [P, NCH, FEAT], F32R)
        count_b = sb("count_b", [P, NCH, NODES], BF16)
        adj = sb("adj", [P, NCH, NODES], F32R)
        degs = sb("degs", [P, 2 * NCH])
        roots = sb("roots", [P, 2 * NCH])
        rsq = sb("rsq", [P, 2 * NCH])
        y_hi = sb("y_hi", [P, NCH, FEAT], F32R)
        y_lo = sb("y_lo", [P, NCH, FEAT], F32R)
        x1 = sb("x1", [P, NCH, FEAT])
        sum1 = sb("sum1", [P, NCH])
        negmean1 = sb("negmean1", [P, NCH])
        sumsq1 = sb("sumsq1", [P, NCH])
        eps_col = sb("eps_col", [P, 1])
        std1 = sb("std1", [P, NCH])
        rstd1 = sb("rstd1", [P, NCH])
        h1 = h0
        H_rest = sb("H_rest", [P, NCH, P])
        H_part = sb("H_part", [P, 3, NCH, P], BF16)
        z_abs = sb("z_abs", [P, GLEN])
        radial_sb = z_abs[0:GROUPS * RADIAL]
        squares = z_abs[:].rearrange("p (c f) -> p c f", c=NCH)
        z_pos = sb("z_pos", [P, GLEN])
        hid = sb("hid", [P, GLEN])
        hid_hi = sb("hid_hi", [P, GLEN], F32R)
        hid_lo = sb("hid_lo", [P, GLEN], F32R)
        w2_sb = sb("w2_sb", [P, GROUPS * 4 * F])
        w2_hi = sb("w2_hi", [P, GROUPS * 4 * F], F32R)
        w2_lo = sb("w2_lo", [P, GROUPS * 4 * F], F32R)
        b2_hi = sb("b2_hi", [2, 4 * F], F32R)
        b2_parts = sb("b2_parts", [2, 4 * F], F32R)
        q = sb("q", [P, TILES, 4])
        QW = sb("QW", [P, TILES, 6, F])
        fil_sb = sb("fil_sb", [P, 2, GROUPS, 3, F])
        early = QW[:].rearrange("p t c f -> p (t c f)")
        gw = early[:, 0:2048].rearrange("p (k n) -> p k n", k=KCH)
        dst_b = early[:, 4096:6144].bitcast(BF16)
        free = D[:].rearrange("p t n -> p (t n)").bitcast(F32)
        M = free[:, 0:2048].rearrange("p (b t m f) -> p b t m f", b=2, t=GROUPS, m=8)
        dot3 = free[:, 2048:2432].rearrange("p (t c f) -> p t c f", t=GROUPS, c=3)
        dot2 = free[:, 2432:2560].rearrange("p (t f) -> p t f", t=GROUPS)
        out_sb = free[:, 2560:3584].rearrange("p (c f) -> p c f", c=NCH)
        h1t = out_sb
        M_hi, M_lo = (part[:].rearrange("p k n -> p (k n)").rearrange("p (b t m f) -> p b t m f", b=2, t=GROUPS, m=8)
                      for part in (gw_hi, gw_lo))
        wvv = sb("wvv", [P, 3, P])
        o2s = sb("o2s", [P, P])
        agg_sb = sb("agg_sb", [P, 2, NODES])
        t_abs, t_exp, t_ln, t_pos = (z_pos[:, i * NODES:(i + 1) * NODES] for i in range(4))

        half = sb("half", [P, 1])
        warm = sb("warm", [P, NODES], BF16)

        in_idx, in_x, in_edge, in_radial, in_w1, in_w2, in_b2 = sems("in_idx in_x in_edge in_radial in_w1 in_w2 in_b2")
        in_gw, in_gw2, in_pack, in_bias, in_dst = sems("in_gw in_gw2 in_pack in_bias in_dst")
        half_ready, eps_ready, warm_ready, iota_ready = sems("half_ready eps_ready warm_ready iota_ready")
        ident_zeroed, ident_ready, identb_ready = sems("ident_zeroed ident_ready identb_ready")
        sign_f_ready, sign_ready = sems("sign_f_ready sign_ready")
        idxb_ready, onehots_ready, dt_ready, sr_ready = sems("idxb_ready onehots_ready dt_ready sr_ready")
        first_onehots_ready, last_onehots_ready = sems("first_onehots_ready last_onehots_ready")
        last_src_ready, = sems("last_src_ready")
        stats_ready, mv_ready, negmean_ready, h0_ready = sems("stats_ready mv_ready negmean_ready h0_ready")
        h0t_done, h0t_ready, h0t_lo_ready = sems("h0t_done h0t_ready h0t_lo_ready")
        gw_hi_ready, gw_lo_ready, y_done, counts_done = sems("gw_hi_ready gw_lo_ready y_done counts_done")
        count_ready, adjsum_done, adj_ready, degs_ready = sems("count_ready adjsum_done adj_ready degs_ready")
        roots_ready, rsq_ready, yhi_ready, ylo_ready = sems("roots_ready rsq_ready yhi_ready ylo_ready")
        conv_done, xb_ready, x1_ready = sems("conv_done xb_ready x1_ready")
        negmean1_ready, sumsq1_ready, std1_ready, rstd1_ready = sems(
            "negmean1_ready sumsq1_ready std1_ready rstd1_ready")
        h1_ready = sems("h1_0_ready h1_1_ready")
        h1t_ready = sems("h1t_0_ready h1t_1_ready")
        h1t_done, h_done, H_rest_ready = sems("h1t_done h_done H_rest_ready")
        H_part_ready = sems("H_part0_ready H_part1_ready H_part2_ready")
        z_done, z_used, z_abs_ready, z_exp_ready, z_ln_ready = sems("z_done z_used z_abs_ready z_exp_ready z_ln_ready")
        hid_ready, hid_hi_ready, hid_lo_ready = sems("hid_ready hid_hi_ready hid_lo_ready")
        w2_hi_ready, w2_lo_ready, b2_hi_ready, b2_ready = sems("w2_hi_ready w2_lo_ready b2_hi_ready b2_ready")
        q_ready, fil_done, filsb_ready, filter1_ready, qw_ready = sems(
            "q_ready fil_done filsb_ready filter1_ready qw_ready")
        gath_done, gath_used, dot_ready, m_ready = sems("gath_done gath_used dot_ready m_ready")
        mhi_ready, mlo_ready, mlo_pool_ready = sems("mhi_ready mlo_ready mlo_pool_ready")
        scat_hi_done, scat_lo_done, agg_done = sems("scat_hi_done scat_lo_done agg_done")
        wvv_zeroed, wvv_done, wvv_ready, o2s_ready, o1s_ready = sems("wvv_zeroed wvv_done wvv_ready o2s_ready o1s_ready")
        agg_ready = sems("agg0_ready agg1_ready")
        os1_done, t_abs_ready, t_exp_ready, t_ln_ready, t_pos_ready = sems(
            "os1_done t_abs_ready t_exp_ready t_ln_ready t_pos_ready")
        fin_done, os2_done, out_ready, out_done = sems("fin_done os2_done out_ready out_done")

        x_v = x.rearrange("(c p) f -> p c f", p=P)
        out_v = out.rearrange("(c p) f -> p c f", p=P)
        gw_v = gcn_w.rearrange("(k p) n -> p k n", p=P)

        block = ctx.enter_context(nc.Block())

        @block.sync
        def _(sp):
            sp.dma_start(idx_i[:], idx).then_inc(in_idx, 16)
            sp.dma_start(w1_sb[:], w1_diag).then_inc(in_w1, 16)
            sp.dma_start(radial_sb, radial).then_inc(in_radial, 16)
            sp.dma_start(x_sb[:], x_v).then_inc(in_x, 16)
            sp.dma_start(edge_sb[:], edge_cols).then_inc(in_edge, 16)
            sp.dma_start(b2_sb[:], b2_rows).then_inc(in_b2, 16)
            sp.dma_start(w2_sb[:], w2_diag).then_inc(in_w2, 16)
            sp.dma_start(gw[:, 0:2], gw_v[:, 0:2]).then_inc(in_gw, 16)
            sp.dma_start(gw[:, 2:4], gw_v[:, 2:4]).then_inc(in_gw2, 16)
            sp.dma_start(bias_sb[:], gcn_b.to_broadcast([P, FEAT])).then_inc(in_bias, 16)
            sp.dma_start(wp[:], w_pack).then_inc(in_pack, 16)
            for c in range(NCH):
                sp.wait_ge(out_ready, c + 1)
                sp.dma_start(out_v[:, c, B:FEAT], out_sb[:, c, B:FEAT]).then_inc(out_done, 16)
            sp.wait_ge(out_ready, NCH + 1)
            sp.dma_start(out_v[:, :, 0:B], out_sb[:, :, 0:B]).then_inc(out_done, 16)
            sp.wait_ge(out_done, 16 * (NCH + 1))

        @block.gpsimd
        def _(pool):
            nc.gpsimd.iota(iota_b[:], [[1, NODES]], base=0, channel_multiplier=0,
                           allow_small_or_imprecise_dtypes=True).then_inc(iota_ready, 1)
            nc.gpsimd.memset(ident_wide[:], 0.0).then_inc(ident_zeroed, 1)
            pool.wait_ge(ident_zeroed, 1)
            nc.gpsimd.affine_select(out=ident_wide[:], in_=ident_wide[:], compare_op=ALU.not_equal, fill=1.0,
                                    base=P, pattern=[[-1, 3 * P]], channel_multiplier=1).then_inc(ident_ready, 1)
            nc.gpsimd.iota(node_id[:], [[P, NCH]], base=0, channel_multiplier=1,
                           allow_small_or_imprecise_dtypes=True).then_inc(iota_ready, 1)
            pool.wait_ge(ident_ready, 1)
            nc.gpsimd.tensor_copy(ident_b[:], ident).then_inc(identb_ready, 1)
            nc.gpsimd.iota(sign_f[:], [[0, P]], base=-1, channel_multiplier=2,
                           allow_small_or_imprecise_dtypes=True).then_inc(sign_f_ready, 1)
            pool.wait_ge(sign_f_ready, 1)
            nc.gpsimd.tensor_copy(sign[:], sign_f[:]).then_inc(sign_ready, 1)
            nc.gpsimd.memset(wvv[:], 0.0).then_inc(wvv_zeroed, 1)
            pool.wait_ge(in_idx, 16)
            nc.gpsimd.tensor_copy(last_src[:], idx_i[:, TILES - GROUPS:TILES]).then_inc(last_src_ready, 1)
            pool.wait_ge(last_src_ready, 1)
            for g in range(GROUPS):
                nc.gpsimd.tensor_scalar(S[:, TILES - GROUPS + g], iota_b[:], last_src[:, g:g + 1], None,
                                        ALU.is_equal).then_inc(last_onehots_ready, 1)
            pool.wait_ge(in_edge, 16)
            nc.gpsimd.tensor_tensor(q[:], edge_sb[:, 0:4 * TILES].rearrange("p (t c) -> p t c", c=4),
                                    edge_sb[:, 4 * TILES:5 * TILES, None].to_broadcast([P, TILES, 4]),
                                    ALU.mult).then_inc(q_ready, 1)
            nc.gpsimd.dma_start(dst_b, dst_row.to_broadcast([P, EDGES])).then_inc(in_dst, 16)
            pool.wait_ge(in_b2, 16)
            pool.wait_ge(b2_hi_ready, 1)
            nc.gpsimd.tensor_tensor(b2_parts[:], b2_sb[:, 1], b2_hi[:].bitcast(F32), ALU.subtract).then_inc(b2_ready, 1)
            pool.wait_ge(w2_hi_ready, 1)
            nc.gpsimd.tensor_tensor(w2_lo[:], w2_sb[:], w2_hi[:].bitcast(F32), ALU.subtract).then_inc(w2_lo_ready, 1)
            for n, ready in enumerate((in_gw, in_gw2)):
                pool.wait_ge(gw_hi_ready, n + 1)
                nc.gpsimd.tensor_tensor(gw_lo[:, 2 * n:2 * n + 2], gw[:, 2 * n:2 * n + 2],
                                        gw_hi[:, 2 * n:2 * n + 2].bitcast(F32), ALU.subtract).then_inc(gw_lo_ready, 1)
            for n in range(2):
                cols = slice(512 * n, 512 * n + 512)
                pool.wait_ge(z_ln_ready, n + 1)
                nc.gpsimd.tensor_tensor(hid[:, cols], z_abs[:, cols], z_pos[:, cols], ALU.add).then_inc(hid_ready, 1)

            def low_of_hidden(n):
                cols = slice(512 * n, 512 * n + 512)
                pool.wait_ge(hid_ready, n + 1)
                pool.wait_ge(hid_hi_ready, n + 1)
                nc.gpsimd.tensor_tensor(hid_lo[:, cols], hid[:, cols], hid_hi[:, cols].bitcast(F32),
                                        ALU.subtract).then_inc(hid_lo_ready, 1)

            low_of_hidden(0)
            pool.wait_ge(in_bias, 16)
            pool.wait_ge(in_x, 16)
            pool.wait_ge(stats_ready, NCH)
            pool.wait_ge(h0_ready, NCH)
            nc.gpsimd.tensor_tensor(x_sb[:], x_sb[:], bias_sb[:, None, :].to_broadcast([P, NCH, FEAT]),
                                    ALU.add).then_inc(xb_ready, 1)
            low_of_hidden(1)
            pool.wait_ge(in_pack, 16)
            nc.gpsimd.tensor_scalar(o2s[:], wp[:, W_O2S:W_O2S + P], OUT_SCALE, None, ALU.mult).then_inc(o2s_ready, 1)
            pool.wait_ge(o2s_ready, 1)
            nc.gpsimd.tensor_scalar(wp[F:2 * F, W_O1S:W_O1S + P], wp[F:2 * F, W_O1S:W_O1S + P], IS3, None,
                                    ALU.mult).then_inc(o1s_ready, 1)
            pool.wait_ge(o1s_ready, 1)
            pool.wait_ge(q_ready, 1)
            pool.wait_ge(gw_lo_ready, 2)

            def filters(k):
                ts = slice(k * GROUPS, (k + 1) * GROUPS)
                pool.wait_ge(filsb_ready, k + 1)
                if k == 5:
                    pool.wait_ge(dt_ready, 2 * NCH)
                nc.gpsimd.tensor_tensor(QW[:, ts, 0:5:4], fil_sb[:, k % 2, :, 0:2],
                                        q[:, ts, 0:1, None].to_broadcast([P, GROUPS, 2, F]),
                                        ALU.mult).then_inc(qw_ready, 1)
                nc.gpsimd.tensor_tensor(QW[:, ts, 1:4], fil_sb[:, k % 2, :, 2:3].to_broadcast([P, GROUPS, 3, F]),
                                        q[:, ts, 1:4, None].to_broadcast([P, GROUPS, 3, F]),
                                        ALU.mult).then_inc(qw_ready, 1)

            for k in range(4):
                filters(k)
            for k in range(CHUNKS):
                pool.wait_ge(mhi_ready, k + 1)
                if k >= 2:
                    pool.wait_ge(scat_lo_done, k - 1)
                gs = slice(LO_DVE[k], GROUPS)
                nc.gpsimd.tensor_tensor(M_lo[:, k % 2, gs], M[:, k % 2, gs], M_hi[:, k % 2, gs].bitcast(F32),
                                        ALU.subtract).then_inc(mlo_pool_ready, 1)
                if k + 4 < CHUNKS:
                    filters(k + 4)

        @block.scalar
        def _(act):
            nc.scalar.preload_act_table_set("natural_log_exp_and_others")
            act.wait_ge(in_edge, 16)
            act.wait_ge(half_ready, 1)
            b1 = edge_sb[:, 5 * TILES:5 * TILES + 1]

            def softplus_from_psum(n):
                cols = slice(512 * n, 512 * n + 512)
                act.wait_ge(z_done, n + 1)
                nc.scalar.activation(z_abs[:, cols], z_ps[n], ACT.Abs, bias=b1).then_inc(z_abs_ready, 1)
                nc.scalar.activation(z_pos[:, cols], z_ps[n], ACT.Relu, bias=b1).then_inc(z_used, 1)

            act.wait_ge(in_b2, 16)
            nc.scalar.copy(b2_hi[:], b2_sb[:, 0]).then_inc(b2_hi_ready, 1)
            act.wait_ge(negmean_ready, 1)
            for c in range(NCH):
                nc.scalar.activation(h0[:, c], x_sb[:, c], ACT.Relu, bias=negmean[:, c:c + 1]).then_inc(h0_ready, 1)
            act.wait_ge(in_w2, 16)
            nc.scalar.copy(w2_hi[:], w2_sb[:]).then_inc(w2_hi_ready, 1)
            for c in range(NCH):
                act.wait_ge(h0t_done, c + 1)
                nc.scalar.copy(h0t_hi[:, c], h0t_ps[c]).then_inc(h0t_ready, 1)
            for n, ready in enumerate((in_gw, in_gw2)):
                act.wait_ge(ready, 16)
                nc.scalar.copy(gw_hi[:, 2 * n:2 * n + 2], gw[:, 2 * n:2 * n + 2]).then_inc(gw_hi_ready, 1)
            softplus_from_psum(0)
            softplus_from_psum(1)
            for n in range(2):
                cols = slice(512 * n, 512 * n + 512)
                act.wait_ge(z_abs_ready, n + 1)
                nc.scalar.activation(z_abs[:, cols], z_abs[:, cols], ACT.Exp, scale=-1.0).then_inc(z_exp_ready, 1)
            for n in range(2):
                cols = slice(512 * n, 512 * n + 512)
                act.wait_ge(z_exp_ready, n + 1)
                nc.scalar.activation(z_abs[:, cols], z_abs[:, cols], ACT.Ln, bias=half[:],
                                     scale=0.5).then_inc(z_ln_ready, 1)
            nc.scalar.preload_act_table_set("sqrt_and_others")

            def scatter_onehots(k):
                if k == 0:
                    act.wait_ge(first_onehots_ready, 2)
                else:
                    act.wait_ge(onehots_ready, k)
                if k == CHUNKS - 1:
                    act.wait_ge(last_onehots_ready, GROUPS)
                ts = slice(k * GROUPS, (k + 1) * GROUPS)
                nc.scalar.copy(S_r[:, ts], S[:, ts]).then_inc(sr_ready, 1)

            def high_of_hidden(n):
                cols = slice(512 * n, 512 * n + 512)
                act.wait_ge(hid_ready, n + 1)
                nc.scalar.copy(hid_hi[:, cols], hid[:, cols]).then_inc(hid_hi_ready, 1)

            act.wait_ge(degs_ready, 2)
            nc.scalar.activation(roots[:], degs[:], ACT.Sqrt).then_inc(roots_ready, 1)
            high_of_hidden(0)
            high_of_hidden(1)

            def filters_out(k):
                fil = fil_ps[k % 2].rearrange("p (t h f) -> p t h f", t=GROUPS, h=4)
                act.wait_ge(fil_done, k + 1)
                if k == 0:
                    act.wait_ge(gw_lo_ready, 2)
                if k == 5:
                    act.wait_ge(dt_ready, 2 * NCH)
                if k >= 2:
                    act.wait_ge(qw_ready, 2 * k - 2)
                nc.scalar.copy(fil_sb[:, k % 2], fil[:, :, 0:3]).then_inc(filsb_ready, 1)
                nc.scalar.copy(QW[:, k * GROUPS:(k + 1) * GROUPS, 5], fil[:, :, 3]).then_inc(filter1_ready, 1)

            for k in range(4):
                scatter_onehots(k)
            act.wait_ge(negmean1_ready, 1)
            nc.scalar.activation(h1[:, 0], x1[:, 0], ACT.Relu, bias=negmean1[:, 0:1]).then_inc(h1_ready[0], 1)
            filters_out(0)
            act.wait_ge(h1t_done, 1)
            nc.scalar.copy(h1t[:, 0], h1t_ps[0]).then_inc(h1t_ready[0], 1)
            for c in range(NCH):
                act.wait_ge(negmean1_ready, c + 1)
                nc.scalar.activation(squares[:, c], x1[:, c], ACT.Square, bias=negmean1[:, c:c + 1],
                                     accum_out=sumsq1[:, c:c + 1]).then_inc(sumsq1_ready, 1)
            act.wait_ge(sumsq1_ready, 2)
            act.wait_ge(eps_ready, 1)
            nc.scalar.activation(std1[:], sumsq1[:], ACT.Sqrt, bias=eps_col[:],
                                 scale=1.0 / (FEAT * H_SCALE ** 2)).then_inc(std1_ready, 1)
            for k in range(1, 5):
                filters_out(k)
            nc.scalar.preload_act_table_set("natural_log_exp_and_others")
            for k in range(CHUNKS):
                act.wait_ge(m_ready, k + 1)
                if k >= 2:
                    act.wait_ge(scat_hi_done, k - 1)
                nc.scalar.copy(M_hi[:, k % 2], M[:, k % 2]).then_inc(mhi_ready, 1)
                if k + 5 < CHUNKS:
                    filters_out(k + 5)
                if k + 4 < CHUNKS:
                    scatter_onehots(k + 4)
            act.wait_ge(wvv_zeroed, 1)
            act.wait_ge(wvv_done, 1)
            nc.scalar.mul(wvv[2 * F:P, 0:3:2], wvv_ps[2 * F:P, None, :].to_broadcast([2 * F, 2, P]),
                          OUT_SCALE).then_inc(wvv_ready, 1)
            nc.scalar.mul(wvv[0:2 * F, 1], wvv_ps[0:2 * F], OUT_SCALE).then_inc(wvv_ready, 1)
            act.wait_ge(agg_done, 1)
            nc.scalar.copy(agg_sb[:, 0], agg_ps[0]).then_inc(agg_ready[0], 1)
            act.wait_ge(os1_done, 1)
            nc.scalar.activation(t_abs, os1_ps, ACT.Abs).then_inc(t_abs_ready, 1)
            act.wait_ge(t_abs_ready, 1)
            nc.scalar.activation(t_exp, t_abs, ACT.Exp, scale=-1.0).then_inc(t_exp_ready, 1)
            act.wait_ge(t_exp_ready, 1)
            nc.scalar.activation(t_ln, t_exp, ACT.Ln, bias=half[:], scale=0.5).then_inc(t_ln_ready, 1)

        @block.vector
        def _(dve):
            nc.vector.memset(warm[:], 0.0).then_inc(warm_ready, 1)
            nc.vector.memset(half[:], 0.5).then_inc(half_ready, 1)
            nc.vector.memset(eps_col[:], LN_EPS / H_SCALE ** 2).then_inc(eps_ready, 1)
            dve.wait_ge(in_idx, 16)
            nc.vector.tensor_copy(idx_b[:], idx_i[:, :, None].to_broadcast([P, 2 * TILES, 2])).then_inc(idxb_ready, 1)
            dve.wait_ge(idxb_ready, 1)
            dve.wait_ge(iota_ready, 1)

            def onehots(side, first, tiles):
                at = side * TILES + first
                return nc.vector.tensor_tensor(
                    (S, D)[side][:, first:first + tiles].rearrange("p t (n two) -> p t n two", two=2),
                    idx_b[:, at:at + tiles, None, :].to_broadcast([P, tiles, NODES // 2, 2]),
                    iota_b[:, None, :].to_broadcast([P, tiles, NODES]).rearrange("p t (n two) -> p t n two", two=2),
                    ALU.is_equal)

            for first in (0, 2):
                onehots(0, first, 2)
                onehots(1, first, 2).then_inc(first_onehots_ready, 1)
            onehots(0, GROUPS, GROUPS)
            onehots(1, GROUPS, GROUPS).then_inc(onehots_ready, 1)
            onehots(0, 2 * GROUPS, GROUPS)
            dve.wait_ge(in_x, 16)
            for c in range(NCH):
                nc.vector.bn_stats(stats[:, c], x_sb[:, c]).then_inc(stats_ready, 1)
            dve.wait_ge(stats_ready, NCH)
            for c in range(NCH):
                nc.vector.bn_aggr(mv[:, c], stats[:, c]).then_inc(mv_ready, 1)
            dve.wait_ge(mv_ready, NCH)
            nc.vector.tensor_scalar(negmean[:], mv[:, :, 0], -1.0, None, ALU.mult).then_inc(negmean_ready, 1)
            for k in range(2, CHUNKS):
                if 2 < k < CHUNKS - 1:
                    onehots(0, k * GROUPS, GROUPS)
                onehots(1, k * GROUPS, GROUPS).then_inc(onehots_ready, 1)

            def low_of_h0t(c):
                dve.wait_ge(h0t_ready, c + 1)
                nc.vector.tensor_tensor(h0t_lo[:, c], h0t_ps[c], h0t_hi[:, c].bitcast(F32),
                                        ALU.subtract).then_inc(h0t_lo_ready, 1)

            def gather_onehots(n):
                edges, c = slice((n // NCH) * 2048, (n // NCH) * 2048 + 2048), n % NCH
                nc.vector.tensor_scalar(DT[:, c, edges], dst_b[:, edges], node_id[:, c:c + 1], None,
                                        ALU.is_equal).then_inc(dt_ready, 1)

            low_of_h0t(0)
            dve.wait_ge(in_dst, 16)
            dve.wait_ge(iota_ready, 2)
            gather_onehots(0)
            dve.wait_ge(counts_done, 1)
            for c in range(NCH):
                nc.vector.tensor_scalar(count_b[:, c], count_ps[c], 1.0, None, ALU.min).then_inc(count_ready, 1)
            low_of_h0t(1)
            gather_onehots(1)
            dve.wait_ge(adjsum_done, 1)
            dve.wait_ge(ident_ready, 1)
            for c in range(NCH):
                nc.vector.scalar_tensor_tensor(out=adj[:, c], in0=adj_ps[c], scalar=1.0,
                                               in1=ident_wide[:, P - P * c:3 * P - P * c], op0=ALU.min, op1=ALU.add,
                                               accum_out=degs[:, c:c + 1]).then_inc(adj_ready, 1)
            dve.wait_ge(adj_ready, NCH)
            nc.vector.scalar_tensor_tensor(out=degs[:, NCH:2 * NCH], in0=mv[:, :, 1], scalar=LN_EPS,
                                           in1=degs[:, 0:NCH], op0=ALU.add, op1=ALU.mult).then_inc(degs_ready, 2)
            dve.wait_ge(roots_ready, 1)
            nc.vector.reciprocal(rsq[:], roots[:]).then_inc(rsq_ready, 1)
            dve.wait_ge(rsq_ready, 1)
            for c in range(NCH):
                dve.wait_ge(y_done, c + 1)
                scale = rsq[:, NCH + c:NCH + c + 1]
                nc.vector.tensor_scalar(y_hi[:, c], y_ps[c], scale, None, ALU.mult).then_inc(yhi_ready, 1)
                dve.wait_ge(yhi_ready, c + 1)
                nc.vector.scalar_tensor_tensor(out=y_lo[:, c], in0=y_ps[c], scalar=scale,
                                               in1=y_hi[:, c].bitcast(F32), op0=ALU.mult,
                                               op1=ALU.subtract).then_inc(ylo_ready, 1)
            dve.wait_ge(xb_ready, 1)
            for c in range(NCH):
                dve.wait_ge(conv_done, c + 1)
                nc.vector.scalar_tensor_tensor(out=x1[:, c], in0=conv_ps[c], scalar=rsq[:, c:c + 1], in1=x_sb[:, c],
                                               op0=ALU.mult, op1=ALU.add,
                                               accum_out=sum1[:, c:c + 1]).then_inc(x1_ready, 1)
                dve.wait_ge(x1_ready, c + 1)
                nc.vector.tensor_scalar(negmean1[:, c:c + 1], sum1[:, c:c + 1], -1.0 / FEAT, None,
                                        ALU.mult).then_inc(negmean1_ready, 1)
            dve.wait_ge(negmean1_ready, 2)
            nc.vector.tensor_scalar(h1[:, 1], x1[:, 1], negmean1[:, 1:2], 0.0, ALU.add, ALU.max).then_inc(h1_ready[1], 1)
            gather_onehots(2)
            dve.wait_ge(h1t_done, 2)
            nc.vector.tensor_copy(h1t[:, 1], h1t_ps[1]).then_inc(h1t_ready[1], 1)
            gather_onehots(3)
            dve.wait_ge(std1_ready, 1)
            nc.vector.reciprocal(rstd1[:], std1[:]).then_inc(rstd1_ready, 1)
            dve.wait_ge(rstd1_ready, 1)
            for c in range(NCH):
                dve.wait_ge(h_done, c + 1)
                nc.vector.tensor_scalar(H_part[:, 0, c], h_ps[c], rstd1[:, c:c + 1], None,
                                        ALU.mult).then_inc(H_part_ready[0], 1)
            for c in range(NCH):
                dve.wait_ge(H_part_ready[0], c + 1)
                nc.vector.scalar_tensor_tensor(out=H_rest[:, c], in0=h_ps[c], scalar=rstd1[:, c:c + 1],
                                               in1=H_part[:, 0, c], op0=ALU.mult,
                                               op1=ALU.subtract).then_inc(H_rest_ready, 1)
            for c in range(NCH):
                dve.wait_ge(H_rest_ready, c + 1)
                nc.vector.tensor_copy(H_part[:, 1, c], H_rest[:, c]).then_inc(H_part_ready[1], 1)
            for c in range(NCH):
                dve.wait_ge(H_part_ready[1], c + 1)
                nc.vector.tensor_tensor(H_part[:, 2, c], H_rest[:, c], H_part[:, 1, c],
                                        ALU.subtract).then_inc(H_part_ready[2], 1)

            def low_parts(k):
                b = k % 2
                dve.wait_ge(mhi_ready, k + 1)
                if k >= 2:
                    dve.wait_ge(scat_lo_done, k - 1)
                gs = slice(0, LO_DVE[k])
                nc.vector.tensor_tensor(M_lo[:, b, gs], M[:, b, gs], M_hi[:, b, gs].bitcast(F32),
                                        ALU.subtract).then_inc(mlo_ready, 1)

            def messages(k):
                ts = slice(k * GROUPS, (k + 1) * GROUPS)
                b = k % 2
                gath = gath_ps[b].rearrange("p (t c f) -> p t c f", t=GROUPS, c=4)
                dve.wait_ge(gath_done, k + 1)
                if k == 0:
                    dve.wait_ge(q_ready, 1)
                if k >= 2:
                    dve.wait_ge(mlo_ready, k - 1)
                    dve.wait_ge(mlo_pool_ready, k - 1)
                if k >= 1:
                    dve.wait_ge(m_ready, k)
                nc.vector.tensor_tensor(dot3, gath[:, :, 1:4], q[:, ts, 1:4, None].to_broadcast([P, GROUPS, 3, F]),
                                        ALU.mult).then_inc(dot_ready, 1)
                dve.wait_ge(qw_ready, 2 * k + 2)
                nc.vector.tensor_tensor(M[:, b, :, 3:8:2], gath[:, :, 1:4],
                                        QW[:, ts, 4:5].to_broadcast([P, GROUPS, 3, F]), ALU.mult)
                dve.wait_ge(dot_ready, 3 * k + 1)
                nc.vector.tensor_tensor(dot2, dot3[:, :, 0], dot3[:, :, 1], ALU.add).then_inc(dot_ready, 1)
                nc.vector.tensor_tensor(M[:, b, :, 0:8:2], gath[:, :, 0:1].to_broadcast([P, GROUPS, 4, F]),
                                        QW[:, ts, 0:4], ALU.mult).then_inc(gath_used, 1)
                dve.wait_ge(dot_ready, 3 * k + 2)
                nc.vector.tensor_tensor(dot2, dot2, dot3[:, :, 2], ALU.add).then_inc(dot_ready, 1)
                if k >= 1:
                    low_parts(k - 1)
                dve.wait_ge(dot_ready, 3 * k + 3)
                dve.wait_ge(filter1_ready, k + 1)
                nc.vector.tensor_tensor(M[:, b, :, 1], dot2, QW[:, ts, 5], ALU.mult).then_inc(m_ready, 1)

            for k in range(CHUNKS):
                messages(k)
            low_parts(CHUNKS - 1)
            dve.wait_ge(agg_done, 2)
            nc.vector.tensor_copy(agg_sb[:, 1], agg_ps[1]).then_inc(agg_ready[1], 1)
            dve.wait_ge(t_abs_ready, 1)
            nc.vector.tensor_scalar(t_pos, os1_ps, 0.0, None, ALU.max).then_inc(t_pos_ready, 1)

            def vector_parts(c):
                dve.wait_ge(fin_done, c + 1)
                nc.vector.tensor_tensor(out_sb[:, c, B:FEAT].rearrange("p (d c) -> p d c", c=3),
                                        fin_ps[c][:, B:FEAT].rearrange("p (c d) -> p d c", c=3),
                                        x1[:, c, B:FEAT].rearrange("p (d c) -> p d c", c=3),
                                        ALU.add).then_inc(out_ready, 1)

            vector_parts(0)
            vector_parts(1)
            for c in range(NCH):
                dve.wait_ge(os2_done, c + 1)
                last = nc.vector.tensor_tensor(out_sb[:, c, 0:B], os2_ps[c], x1[:, c, 0:B], ALU.add)
            last.then_inc(out_ready, 1)

        @block.tensor
        def _(pe):
            def count(k):
                if k > 0:
                    pe.wait_ge(onehots_ready, k)
                if k == CHUNKS - 1:
                    pe.wait_ge(last_onehots_ready, GROUPS)
                for g in range(GROUPS):
                    t = k * GROUPS + g
                    if k == 0 and g % 2 == 0:
                        pe.wait_ge(first_onehots_ready, g // 2 + 1)
                    for c in range(NCH):
                        last = nc.tensor.matmul(count_ps[c], S[:, t, c * P:(c + 1) * P], D[:, t],
                                                start=t == 0, stop=t == TILES - 1)
                if k == CHUNKS - 1:
                    last.then_inc(counts_done, 1)

            pe.wait_ge(warm_ready, 1)
            for _ in range(WARM_UP):
                nc.tensor.matmul(z_ps[1][:, 0:NODES], warm[:, 0:P], warm[:], start=True, stop=True)
            count(0)
            pe.wait_ge(in_w1, 16)
            pe.wait_ge(in_radial, 16)
            for n in range(2):
                nc.tensor.matmul(z_ps[n], w1_sb[:], radial_sb[:, 512 * n:512 * n + 512], start=True,
                                 stop=True).then_inc(z_done, 1)
            count(1)
            pe.wait_ge(ident_ready, 1)
            for c in range(NCH):
                pe.wait_ge(h0_ready, c + 1)
                for k in range(KCH):
                    last = nc.tensor.transpose(h0t_ps[c][:, k * P:(k + 1) * P], h0[:, c, k * P:(k + 1) * P], ident)
                last.then_inc(h0t_done, 1)
            for k in range(2, CHUNKS):
                count(k)

            def convolve_weights(c, n):
                pe.wait_ge(h0t_ready, c + 1)
                pe.wait_ge(gw_hi_ready, 2)
                if n == 1:
                    pe.wait_ge(h0t_lo_ready, c + 1)
                if n == 2:
                    pe.wait_ge(gw_lo_ready, 2)
                a, b = ((h0t_hi, gw_hi), (h0t_lo, gw_hi), (h0t_hi, gw_lo))[n]
                for k in range(KCH):
                    last = nc.tensor.matmul(y_ps[c], a[:, c, k * P:(k + 1) * P], b[:, k], start=n == 0 and k == 0,
                                            stop=n == 2 and k == KCH - 1)
                if n == 2:
                    last.then_inc(y_done, 1)

            convolve_weights(0, 0)
            convolve_weights(0, 1)
            pe.wait_ge(h0t_lo_ready, 2)
            pe.wait_ge(count_ready, 2)
            pe.wait_ge(identb_ready, 1)
            for c in range(NCH):
                nc.tensor.matmul(adj_ps[c], ident_b[:], count_b[:, c], start=True, stop=False)
                for j in range(NCH):
                    last = nc.tensor.matmul(adj_ps[c][:, j * P:(j + 1) * P], count_b[:, j, c * P:(c + 1) * P],
                                            ident_b[:], start=False, stop=j == NCH - 1)
            last.then_inc(adjsum_done, 1)
            convolve_weights(0, 2)
            for n in range(3):
                convolve_weights(1, n)

            def convolve(j):
                for part in (y_hi, y_lo):
                    pe.wait_ge(yhi_ready if part is y_hi else ylo_ready, j + 1)
                    for c in range(NCH):
                        last = nc.tensor.matmul(conv_ps[c], adj[:, j, c * P:(c + 1) * P], part[:, j],
                                                start=j == 0 and part is y_hi, stop=j == NCH - 1 and part is y_lo)
                        if j == NCH - 1 and part is y_lo:
                            last.then_inc(conv_done, 1)

            def filter_out(k):
                pe.wait_ge(hid_hi_ready, k // 4 + 1)
                pe.wait_ge(hid_lo_ready, k // 4 + 1)
                if k == 0:
                    pe.wait_ge(z_used, 2)
                    pe.wait_ge(w2_hi_ready, 1)
                    pe.wait_ge(w2_lo_ready, 1)
                    pe.wait_ge(b2_ready, 1)
                    pe.wait_ge(sign_ready, 1)
                if k >= 2:
                    pe.wait_ge(filter1_ready, k - 1)
                for n, (a, b) in enumerate(((hid_hi, w2_hi), (hid_lo, w2_hi), (hid_hi, w2_lo))):
                    nc.tensor.matmul(fil_ps[k % 2], a[:, k * P:(k + 1) * P], b[:], start=n == 0, stop=False)
                nc.tensor.matmul(fil_ps[k % 2], sign[:], b2_parts[:, None, :].to_broadcast([2, GROUPS, 4 * F]),
                                 start=False, stop=True).then_inc(fil_done, 1)

            convolve(0)
            convolve(1)
            filter_out(0)
            filter_out(1)
            pe.wait_ge(in_pack, 16)
            pe.wait_ge(ylo_ready, 2)
            nc.tensor.matmul(wvv_ps, wp[:, W_O1VT:W_O1VT + P], wp[:, W_O2V:W_O2V + P], start=True,
                             stop=True).then_inc(wvv_done, 1)
            for c in range(NCH):
                pe.wait_ge(h1_ready[c], 1)
                for n in range(4):
                    part = h1[:, c, 0:B] if n == 0 else h1[:, c, B + n - 1:FEAT:3]
                    last = nc.tensor.transpose(h1t_ps[c][:, n * P:(n + 1) * P], part, ident)
                last.then_inc(h1t_done, 1)
            filter_out(2)
            for c in range(NCH):
                pe.wait_ge(h1t_ready[c], 1)
                for n in range(4):
                    w = wp[:, W_IN_S:W_IN_S + F] if n == 0 else wp[:, W_IN_V:W_IN_V + F]
                    last = nc.tensor.matmul(h_ps[c][:, n * F:(n + 1) * F],
                                            h1t[:, c, n * P:(n + 1) * P], w, start=True, stop=True)
                last.then_inc(h_done, 1)
            filter_out(3)
            filter_out(4)

            def gather(k):
                if k == 0:
                    pe.wait_ge(H_part_ready[2], NCH)
                    pe.wait_ge(dt_ready, 2 * NCH)
                if k >= 2:
                    pe.wait_ge(gath_used, k - 1)
                for g in range(GROUPS):
                    t = k * GROUPS + g
                    for n in range(3 * NCH):
                        c, part = n % NCH, n // NCH
                        last = nc.tensor.matmul(gath_ps[k % 2][:, g * P:(g + 1) * P], DT[:, c, t * P:(t + 1) * P],
                                                H_part[:, part, c], start=n == 0, stop=n == 3 * NCH - 1)
                last.then_inc(gath_done, 1)

            def scatter(k, part, halves=(0, 1)):
                if part is M_hi:
                    pe.wait_ge(mhi_ready, k + 1)
                    pe.wait_ge(sr_ready, k + 1)
                else:
                    pe.wait_ge(mlo_ready, k + 1)
                    pe.wait_ge(mlo_pool_ready, k + 1)
                for rows_half in halves:
                    for g in range(GROUPS):
                        t = k * GROUPS + g
                        rows = part[:, k % 2, g, 4 * rows_half:4 * rows_half + 4].rearrange("p m f -> p (m f)")
                        last = nc.tensor.matmul(agg_ps[rows_half], rows, S_r[:, t],
                                                start=t == 0 and part is M_hi,
                                                stop=t == TILES - 1 and part is M_lo)
                return last

            gather(0)
            gather(1)
            filter_out(5)
            for k in range(CHUNKS):
                if k + 2 < CHUNKS:
                    gather(k + 2)
                if k >= 1:
                    scatter(k - 1, M_lo).then_inc(scat_lo_done, 1)
                if k < CHUNKS - 1:
                    scatter(k, M_hi).then_inc(scat_hi_done, 1)
                if k + 6 < CHUNKS:
                    filter_out(k + 6)
            for rows_half in range(2):
                scatter(CHUNKS - 1, M_hi, (rows_half,))
                scatter(CHUNKS - 1, M_lo, (rows_half,)).then_inc(agg_done, 1)
            pe.wait_ge(agg_ready[0], 1)
            pe.wait_ge(o1s_ready, 1)
            nc.tensor.matmul(os1_ps, wp[:, W_O1S:W_O1S + P], agg_sb[:, 0], start=True,
                             stop=True).then_inc(os1_done, 1)
            pe.wait_ge(wvv_ready, 2)
            for c in range(NCH):
                nc.tensor.matmul(fin_ps[c][:, B:2 * B], agg_sb[:, 0, c * P:(c + 1) * P], wvv[:, 0], start=True,
                                 stop=True)
            pe.wait_ge(agg_ready[1], 1)
            for c in range(NCH):
                nc.tensor.matmul(fin_ps[c][:, 2 * B:4 * B], agg_sb[:, 1, c * P:(c + 1) * P],
                                 wvv[:, 1:3].rearrange("p d n -> p (d n)"), start=True,
                                 stop=True).then_inc(fin_done, 1)
            pe.wait_ge(o2s_ready, 1)
            for term, ready in ((t_pos, t_pos_ready), (t_ln, t_ln_ready)):
                pe.wait_ge(ready, 1)
                for c in range(NCH):
                    last = nc.tensor.matmul(os2_ps[c], term[:, c * P:(c + 1) * P], o2s[:], start=term is t_pos,
                                            stop=term is t_ln)
                    if term is t_ln:
                        last.then_inc(os2_done, 1)


_INS = ["x", "idx", "dst_row", "edge_cols", "radial", "w1_diag", "w2_diag", "b2_rows", "w_pack", "gcn_w", "gcn_b"]


def lay_out(i):
    import numpy as np

    def tiles(a):
        a = np.asarray(a)
        a = a.reshape((GROUPS, CHUNKS, P) + a.shape[1:])
        a = np.moveaxis(a, (2, 1, 0), (0, 1, 2))
        return np.ascontiguousarray(a.reshape((P, TILES) + a.shape[3:]))

    src, dst = np.asarray(i["src"]), np.asarray(i["dst"])
    w1 = np.asarray(i["L1_gnn_W1"])
    w1_diag = np.zeros((GROUPS * RADIAL, P), w1.dtype)
    for g in range(GROUPS):
        w1_diag[g * RADIAL:(g + 1) * RADIAL, g * F:(g + 1) * F] = w1
    w2 = np.asarray(i["L1_gnn_W2"]).reshape(F, F, 6)[:, :, list(FIL_ORDER)]
    w2 = w2.transpose(0, 2, 1).reshape(F, 4 * F)
    w2_diag = np.zeros((P, GROUPS * 4 * F), w2.dtype)
    for g in range(GROUPS):
        w2_diag[g * F:(g + 1) * F, g * 4 * F:(g + 1) * 4 * F] = w2
    b2 = np.asarray(i["L1_gnn_b2"]).reshape(F, 6)[:, list(FIL_ORDER)].T.reshape(4 * F)
    b2_rows = np.zeros((2, 2, 4 * F), b2.dtype)
    b2_rows[:, 0] = b2
    b2_rows[1, 1] = b2
    pack = np.zeros((P, W_PACK), w1.dtype)
    pack[:, W_IN_S:W_IN_S + F] = i["L1_gnn_w_in2f_s"]
    pack[:, W_IN_V:W_IN_V + F] = i["L1_gnn_w_in2f_v"]
    pack[:, W_O1VT:W_O1VT + P] = np.tile(np.asarray(i["L1_gnn_w_f2o1_v"]).T, (1, 2))
    pack[:, W_O2V:W_O2V + P] = i["L1_gnn_w_f2o2_v"]
    pack[:, W_O2S:W_O2S + P] = i["L1_gnn_w_f2o2_s"]
    pack[0:2 * F, W_O1S:W_O1S + P] = i["L1_gnn_w_f2o1_s"]
    return {
        "x": np.asarray(i["x"]),
        "idx": np.concatenate([tiles(src), tiles(dst)], axis=1),
        "dst_row": dst.reshape(GROUPS, CHUNKS, P).transpose(1, 0, 2).reshape(1, EDGES),
        "edge_cols": np.concatenate([tiles(i["edge_attr_4"]).reshape(P, 4 * TILES), tiles(i["edge_weight"]),
                                     np.tile(np.asarray(i["L1_gnn_b1"]), GROUPS)[:, None]], axis=1),
        "radial": np.asarray(i["edge_attr_20"]).reshape(GROUPS, GLEN, RADIAL).transpose(0, 2, 1).reshape(-1, GLEN),
        "w1_diag": w1_diag,
        "w2_diag": w2_diag,
        "b2_rows": b2_rows,
        "w_pack": pack,
        "gcn_w": np.asarray(i["L0_gnn_weight"]),
        "gcn_b": np.asarray(i["L0_gnn_bias"]).reshape(1, FEAT),
    }


def kernel(**inputs):
    import numpy as np
    import concourse.bacc as bacc
    from concourse.bass_utils import run_bass_kernel_spmd

    nc = bacc.Bacc("TRN2", target_bir_lowering=False, num_devices=1)
    laid = lay_out(inputs)
    arrays, args = {}, []
    for name in _INS:
        a = np.ascontiguousarray(laid[name])
        arrays[f"in_{name}"] = a
        args.append(nc.dram_tensor(f"in_{name}", a.shape, mybir.dt.from_np(a.dtype), kind="ExternalInput").ap())
    out = nc.dram_tensor("out_x", (NODES, FEAT), F32, kind="ExternalOutput").ap()
    gnn_kernel(nc, *args, out)
    r = run_bass_kernel_spmd(nc, [arrays], core_ids=[0])
    return r.results[0]["out_x"]
```
